# Optimizing a Trainium2 kernel written in Bass

```python
import numpy as np
import jax
import jax.numpy as jnp

def _softmax(x, axis=-1):
    return jax.nn.softmax(x, axis=axis)

def _gelu(x):
    return jax.nn.gelu(x, approximate=True)

def _silu(x):
    return jax.nn.silu(x)

def _sigmoid(x):
    return jax.nn.sigmoid(x)

def _layernorm(x, axis=-1, eps=1e-05):
    m = jnp.mean(x, axis=axis, keepdims=True)
    v = jnp.var(x, axis=axis, keepdims=True)
    return (x - m) / jnp.sqrt(v + eps)

def _scatter_add(tgt, idx, src, axis=0):
    return tgt.at[idx].add(src)

def _segment_sum(src, seg, n):
    return jax.ops.segment_sum(src, seg, n)
kernel_name = 'mk_gnn_ffn_d2_gnn_r8_d1d545'

def setup_inputs(seed: int=0):
    np.random.seed(seed)
    _w = jnp.asarray

    def _rec_inputs():
        import jax
        import jax.numpy as jnp
        _gk = jax.random.key(seed)
        x = -0.0002928 + 1 * jax.random.normal(jax.random.fold_in(_gk, 1), (1024, 512), jnp.float32)
        _s = jax.random.randint(jax.random.fold_in(_gk, 2), (8192,), 0, 1024, jnp.int32)
        _d = jax.random.randint(jax.random.fold_in(_gk, 3), (8192,), 0, 1024, jnp.int32)
        _loop = jnp.arange(1024, dtype=jnp.int32)
        src = jnp.concatenate([_s, _d, _loop])
        dst = jnp.concatenate([_d, _s, _loop])
        _o = jnp.argsort(dst, stable=True)
        src = src[_o]
        dst = dst[_o]
        return (x, src, dst)
    x, src, dst = _rec_inputs()

    def _L0_gnn_setup():
        import jax, jax.numpy as jnp
        import numpy as np
        NEG = -1000000.0
        key = jax.random.key(seed)
        ks = jax.random.split(key, 8)
        N, D_IN, D_Q, D_K, E = (1024, 512, 512, 512, 32768)
        s = 1.0 / np.sqrt(D_IN)
        return {'x': jax.random.normal(ks[0], (N, D_IN), dtype=jnp.float32), 'edge_index': jax.random.randint(ks[1], (2, E), 0, N, dtype=jnp.int64), 'Wq': jax.random.normal(ks[2], (D_IN, D_Q), dtype=jnp.float32) * s, 'bq': jax.random.normal(ks[3], (D_Q,), dtype=jnp.float32) * 0.01, 'Wk': jax.random.normal(ks[4], (D_IN, D_K), dtype=jnp.float32) * s, 'bk': jax.random.normal(ks[5], (D_K,), dtype=jnp.float32) * 0.01, 'Wv': jax.random.normal(ks[6], (D_IN, D_K), dtype=jnp.float32) * s, 'bv': jax.random.normal(ks[7], (D_K,), dtype=jnp.float32) * 0.01}
    _L0_gnn_all = _L0_gnn_setup()
    _L0_gnn_in = {k: v for k, v in _L0_gnn_all.items() if k in ('Wq', 'bq', 'Wk', 'bk', 'Wv', 'bv')}
    del _L0_gnn_all

    def _L0_ffn_setup():
        import jax, jax.numpy as jnp
        import numpy as np
        TOP_K = 2
        key = jax.random.key(seed)
        ks = jax.random.split(key, 4)
        B, S, D, H, E = (2, 512, 512, 256, 8)
        scale_in = 1.0 / np.sqrt(D)
        scale_h = 1.0 / np.sqrt(H)
        return {'x': jax.random.normal(ks[0], (B, S, D), dtype=jnp.float32), 'gate_w': jax.random.normal(ks[1], (D, E), dtype=jnp.float32) * scale_in, 'gate_b': jnp.zeros((E,), dtype=jnp.float32), 'w1': jax.random.normal(ks[2], (E, D, H), dtype=jnp.float32) * scale_in, 'b1': jnp.zeros((E, H), dtype=jnp.float32), 'w2': jax.random.normal(ks[3], (E, H, D), dtype=jnp.float32) * scale_h, 'b2': jnp.zeros((E, D), dtype=jnp.float32)}
    _L0_ffn_all = _L0_ffn_setup()
    _L0_ffn_in = {k: v for k, v in _L0_ffn_all.items() if k in ('gate_w', 'gate_b', 'w1', 'b1', 'w2', 'b2')}
    del _L0_ffn_all

    def _L1_gnn_setup():
        import jax, jax.numpy as jnp
        import numpy as np
        N_NODES = 1250
        N_EDGES = 20000
        D_IN = 512
        D_HID = 1024
        key = jax.random.key(seed)
        ks = jax.random.split(key, 8)
        feat = jax.random.normal(ks[0], (N_NODES, D_IN), dtype=jnp.float32)
        W1 = jax.random.normal(ks[1], (D_IN, D_HID), dtype=jnp.float32) * (1.0 / np.sqrt(D_IN))
        b1 = jnp.zeros((D_HID,), dtype=jnp.float32)
        W2 = jax.random.normal(ks[2], (D_HID, D_IN), dtype=jnp.float32) * (1.0 / np.sqrt(D_HID))
        b2 = jnp.zeros((D_IN,), dtype=jnp.float32)
        eps = jnp.zeros((1,), dtype=jnp.float32)
        src = jax.random.randint(ks[3], (N_EDGES,), 0, N_NODES, dtype=jnp.int32)
        dst = jax.random.randint(ks[4], (N_EDGES,), 0, N_NODES, dtype=jnp.int32)
        return {'feat': feat, 'W1': W1, 'b1': b1, 'W2': W2, 'b2': b2, 'eps': eps, 'src': src, 'dst': dst}
    _L1_gnn_all = _L1_gnn_setup()
    _L1_gnn_in = {k: v for k, v in _L1_gnn_all.items() if k in ('W1', 'b1', 'W2', 'b2', 'eps')}
    del _L1_gnn_all

    def _L1_ffn_setup():
        import jax, jax.numpy as jnp
        import numpy as np
        D, NH, HID, E = (512, 8, 256, 8)
        EPS = 1e-05

        def _layernorm(x, g, b):
            mu = jnp.mean(x, axis=-1, keepdims=True)
            var = jnp.mean(jnp.square(x - mu), axis=-1, keepdims=True)
            return (x - mu) * jax.lax.rsqrt(var + EPS) * g + b
        key = jax.random.key(seed)
        ks = jax.random.split(key, 20)
        s = 0.02
        inp = {'x': jax.random.normal(ks[0], (4, 1024, D), jnp.float32), 'Wq': jax.random.normal(ks[1], (D, D), jnp.float32) * s, 'bq': jnp.zeros((D,), jnp.float32), 'Wk': jax.random.normal(ks[2], (D, D), jnp.float32) * s, 'bk': jnp.zeros((D,), jnp.float32), 'Wv': jax.random.normal(ks[3], (D, D), jnp.float32) * s, 'bv': jnp.zeros((D,), jnp.float32), 'Wo': jax.random.normal(ks[4], (D, D), jnp.float32) * s, 'bo': jnp.zeros((D,), jnp.float32), 'g1': jnp.ones((D,), jnp.float32), 'beta1': jnp.zeros((D,), jnp.float32), 'g2': jnp.ones((D,), jnp.float32), 'beta2': jnp.zeros((D,), jnp.float32), 'Wg': jax.random.normal(ks[5], (D, E), jnp.float32) * s, 'bg': jnp.zeros((E,), jnp.float32), 'W1': jax.random.normal(ks[6], (E, D, HID), jnp.float32) * s, 'b1': jnp.zeros((E, HID), jnp.float32), 'W2': jax.random.normal(ks[7], (E, HID, D), jnp.float32) * s, 'b2': jnp.zeros((E, D), jnp.float32)}
        return inp
    _L1_ffn_all = _L1_ffn_setup()
    _L1_ffn_in = {k: v for k, v in _L1_ffn_all.items() if k in ('Wq', 'bq', 'Wk', 'bk', 'Wv', 'bv', 'Wo', 'bo', 'g1', 'beta1', 'g2', 'beta2', 'Wg', 'bg', 'W1', 'b1', 'W2', 'b2')}
    del _L1_ffn_all
    return {'x': x, 'src': src, 'dst': dst, 'L0_gnn_Wq': _L0_gnn_in['Wq'], 'L0_gnn_bq': _L0_gnn_in['bq'], 'L0_gnn_Wk': _L0_gnn_in['Wk'], 'L0_gnn_bk': _L0_gnn_in['bk'], 'L0_gnn_Wv': _L0_gnn_in['Wv'], 'L0_gnn_bv': _L0_gnn_in['bv'], 'L0_ffn_gate_w': _L0_ffn_in['gate_w'], 'L0_ffn_gate_b': _L0_ffn_in['gate_b'], 'L0_ffn_w1': _L0_ffn_in['w1'], 'L0_ffn_b1': _L0_ffn_in['b1'], 'L0_ffn_w2': _L0_ffn_in['w2'], 'L0_ffn_b2': _L0_ffn_in['b2'], 'L1_gnn_W1': _L1_gnn_in['W1'], 'L1_gnn_b1': _L1_gnn_in['b1'], 'L1_gnn_W2': _L1_gnn_in['W2'], 'L1_gnn_b2': _L1_gnn_in['b2'], 'L1_gnn_eps': _L1_gnn_in['eps'], 'L1_ffn_Wq': _L1_ffn_in['Wq'], 'L1_ffn_bq': _L1_ffn_in['bq'], 'L1_ffn_Wk': _L1_ffn_in['Wk'], 'L1_ffn_bk': _L1_ffn_in['bk'], 'L1_ffn_Wv': _L1_ffn_in['Wv'], 'L1_ffn_bv': _L1_ffn_in['bv'], 'L1_ffn_Wo': _L1_ffn_in['Wo'], 'L1_ffn_bo': _L1_ffn_in['bo'], 'L1_ffn_g1': _L1_ffn_in['g1'], 'L1_ffn_beta1': _L1_ffn_in['beta1'], 'L1_ffn_g2': _L1_ffn_in['g2'], 'L1_ffn_beta2': _L1_ffn_in['beta2'], 'L1_ffn_Wg': _L1_ffn_in['Wg'], 'L1_ffn_bg': _L1_ffn_in['bg'], 'L1_ffn_W1': _L1_ffn_in['W1'], 'L1_ffn_b1': _L1_ffn_in['b1'], 'L1_ffn_W2': _L1_ffn_in['W2'], 'L1_ffn_b2': _L1_ffn_in['b2']}

def reference(x, src, dst, L0_gnn_Wq, L0_gnn_bq, L0_gnn_Wk, L0_gnn_bk, L0_gnn_Wv, L0_gnn_bv, L0_ffn_gate_w, L0_ffn_gate_b, L0_ffn_w1, L0_ffn_b1, L0_ffn_w2, L0_ffn_b2, L1_gnn_W1, L1_gnn_b1, L1_gnn_W2, L1_gnn_b2, L1_gnn_eps, L1_ffn_Wq, L1_ffn_bq, L1_ffn_Wk, L1_ffn_bk, L1_ffn_Wv, L1_ffn_bv, L1_ffn_Wo, L1_ffn_bo, L1_ffn_g1, L1_ffn_beta1, L1_ffn_g2, L1_ffn_beta2, L1_ffn_Wg, L1_ffn_bg, L1_ffn_W1, L1_ffn_b1, L1_ffn_W2, L1_ffn_b2):
    import jax
    import jax.numpy as jnp

    def _L0_gnn_ref(x, edge_index, Wq, bq, Wk, bk, Wv, bv):
        import jax, jax.numpy as jnp
        import numpy as np
        NEG = -1000000.0
        q = x @ Wq + bq
        k = x @ Wk + bk
        v = x @ Wv + bv
        N = x.shape[0]
        adj = jnp.zeros((N, N), dtype=x.dtype).at[edge_index[0], edge_index[1]].set(1.0)
        a = q @ k.T / jnp.sqrt(jnp.asarray(q.shape[-1], dtype=x.dtype))
        a = a * adj + (1.0 - adj) * NEG
        attn = jax.nn.softmax(a, axis=-1)
        return attn @ v

    def _L0_ffn_ref(x, gate_w, gate_b, w1, b1, w2, b2):
        import jax, jax.numpy as jnp
        import numpy as np
        TOP_K = 2
        B, S, D = x.shape
        E = gate_w.shape[1]
        flat_x = x.reshape(-1, D)
        gate_logits = flat_x @ gate_w + gate_b
        raw_weights = jax.nn.softmax(gate_logits, axis=-1)
        top_w, top_idx = jax.lax.top_k(raw_weights, TOP_K)
        one_hot = jax.nn.one_hot(top_idx, E, dtype=flat_x.dtype)
        gate_output = (one_hot * top_w[..., None]).sum(axis=-2)
        h = jax.nn.gelu(jnp.einsum('td,edh->teh', flat_x, w1) + b1, approximate=False)
        expert_out = jnp.einsum('teh,ehd->ted', h, w2) + b2
        combined = jnp.einsum('ted,te->td', expert_out, gate_output)
        return combined.reshape(B, S, -1)

    def _L1_gnn_ref(feat, W1, b1, W2, b2, eps, src, dst):
        import jax, jax.numpy as jnp
        import numpy as np
        N_NODES = 1250
        N_EDGES = 20000
        D_IN = 512
        D_HID = 1024
        msgs = feat[src]
        neigh = jax.ops.segment_sum(msgs, dst, num_segments=feat.shape[0])
        rst = (1.0 + eps[0]) * feat + neigh
        h = jnp.maximum(rst @ W1 + b1, 0.0)
        h = h @ W2 + b2
        return h + feat

    def _L1_ffn_ref(x, Wq, bq, Wk, bk, Wv, bv, Wo, bo, g1, beta1, g2, beta2, Wg, bg, W1, b1, W2, b2):
        import jax, jax.numpy as jnp
        import numpy as np
        D, NH, HID, E = (512, 8, 256, 8)
        EPS = 1e-05

        def _layernorm(x, g, b):
            mu = jnp.mean(x, axis=-1, keepdims=True)
            var = jnp.mean(jnp.square(x - mu), axis=-1, keepdims=True)
            return (x - mu) * jax.lax.rsqrt(var + EPS) * g + b
        B, S, _ = x.shape
        dh = D // NH
        q = (x @ Wq + bq).reshape(B, S, NH, dh)
        k = (x @ Wk + bk).reshape(B, S, NH, dh)
        v = (x @ Wv + bv).reshape(B, S, NH, dh)
        scores = jnp.einsum('bqhd,bkhd->bhqk', q, k) / jnp.sqrt(jnp.float32(dh)).astype(x.dtype)
        attn = jax.nn.softmax(scores, axis=-1)
        ctx = jnp.einsum('bhqk,bkhd->bqhd', attn, v).reshape(B, S, D)
        sa = ctx @ Wo + bo
        x = _layernorm(x + sa, g1, beta1)
        t = x.reshape(-1, D)
        logits = t @ Wg + bg
        idx = jnp.argmax(logits, axis=-1)
        h = jax.nn.gelu(jnp.einsum('td,edh->teh', t, W1) + b1, approximate=False)
        y = jnp.einsum('teh,ehd->ted', h, W2) + b2
        onehot = jax.nn.one_hot(idx, E, dtype=t.dtype)
        moe = jnp.einsum('ted,te->td', y, onehot).reshape(B, S, D)
        return _layernorm(x + moe, g2, beta2)
    edge_index = jnp.stack([src, dst])
    x = x + _L0_gnn_ref(_layernorm(x, axis=-1), edge_index, L0_gnn_Wq, L0_gnn_bq, L0_gnn_Wk, L0_gnn_bk, L0_gnn_Wv, L0_gnn_bv)
    x = x + _L0_ffn_ref(_layernorm(x, axis=-1)[None], L0_ffn_gate_w, L0_ffn_gate_b, L0_ffn_w1, L0_ffn_b1, L0_ffn_w2, L0_ffn_b2)[0]
    x = x + _L1_gnn_ref(_layernorm(x, axis=-1), L1_gnn_W1, L1_gnn_b1, L1_gnn_W2, L1_gnn_b2, L1_gnn_eps, src, dst)
    x = x + _L1_ffn_ref(_layernorm(x, axis=-1)[None], L1_ffn_Wq, L1_ffn_bq, L1_ffn_Wk, L1_ffn_bk, L1_ffn_Wv, L1_ffn_bv, L1_ffn_Wo, L1_ffn_bo, L1_ffn_g1, L1_ffn_beta1, L1_ffn_g2, L1_ffn_beta2, L1_ffn_Wg, L1_ffn_bg, L1_ffn_W1, L1_ffn_b1, L1_ffn_W2, L1_ffn_b2)[0]
    return x

_drawn_inputs = setup_inputs


def setup_inputs(seed=0):
    import zlib

    import numpy as np

    out = dict(_drawn_inputs(seed))
    spreads = {'L0_ffn_gate_b': (0.0, 0.1),
     'L0_ffn_b1': (0.0, 0.1),
     'L0_ffn_b2': (0.0, 0.1),
     'L1_gnn_b1': (0.0, 0.432),
     'L1_gnn_b2': (0.0, 0.292),
     'L1_ffn_bq': (0.0, 0.8),
     'L1_ffn_bk': (0.0, 0.8),
     'L1_ffn_bv': (0.0, 0.709),
     'L1_ffn_bo': (0.0, 0.342),
     'L1_ffn_g1': (1.0, 0.2),
     'L1_ffn_beta1': (0.0, 0.356),
     'L1_ffn_g2': (1.0, 0.2),
     'L1_ffn_beta2': (0.0, 0.389),
     'L1_ffn_bg': (0.0, 0.459),
     'L1_ffn_b1': (0.0, 0.8),
     'L1_ffn_b2': (0.0, 0.395)}
    factors = {'L0_gnn_bq': 8.0,
     'L0_gnn_bk': 8.0,
     'L1_ffn_Wq': 8.0,
     'L1_ffn_Wk': 8.0,
     'L1_ffn_W1': 3.365,
     'L1_ffn_W2': 3.191}
    for name, (base, spread) in spreads.items():
        noise = np.random.default_rng([zlib.crc32(name.encode()), seed]).standard_normal(out[name].shape)
        drawn = base * np.exp(spread * noise) if base else spread * noise
        out[name] = jnp.asarray(drawn.astype(out[name].dtype))
    for name, factor in factors.items():
        out[name] = (out[name] * factor).astype(out[name].dtype)
    return out
```

```python
import concourse.bass as bass
from concourse import mybir

F32 = mybir.dt.float32
F32R = mybir.dt.float32r
F16 = mybir.dt.float16
I32 = mybir.dt.int32
U32 = mybir.dt.uint32
ALU = mybir.AluOpType
ACT = mybir.ActivationFunctionType
X_AXIS = mybir.AxisListType.X
Copy, Identity = ACT.Copy, ACT.Identity

P = 128


def ds(i, n=1):
    return bass.ds(i, n)


def build(nc, a, out, ctx):
    N, D = a["x"].shape
    NE = a["src"].shape[0]
    NT, KT = N // P, D // P
    HALF = N // 2
    EC = NE // P
    NEXP, _, HID = a["L0_ffn_w1"].shape
    HB = HID // P
    GB = a["L1_gnn_W1"].shape[1] // P
    NH, DH = 8, D // 8
    NEG = 1000000.0
    TABLES = 4
    QUADS = EC // 4
    assert EC % 4 == 0 and HB == 2 and GB == 8 and NT == 8 and KT == 4

    place = [((nc.sbuf_base + 31) // 32) * 32]

    def const(name, shape, dt):
        size = 2 if dt == F16 else 4
        for s in shape[1:]:
            size *= s
        t = nc.alloc_sbuf_tensor_at(name, shape, dt, offset=place[0])
        place[0] += (size + 31) // 32 * 32
        return t

    ident = const("ident", [P, P], F32)
    ident16 = const("ident16", [P, P], F16)
    ident1024 = const("ident1024", [P, P], F16)
    earlier = const("earlier", [P, P], F32)
    spare = const("spare", [P, 1], F32)
    index_s = const("index_s", [P, 2, 4], U32)
    count_s = const("count_s", [P, 2, 4], F32)
    stats = const("stats", [P, NT, 6], F32)
    mv = const("mv", [P, NT, 2], F32)
    ve, rstd, inv, sq = (const(n, [P, NT], F32) for n in ("ve", "rstd", "inv", "sq"))
    bq0 = const("bq0", [P, KT], F32)
    bk0 = const("bk0", [P, KT], F32)
    b1_0 = const("b1_0", [P, NEXP * HB], F32)
    gb1 = const("gb1", [P, GB], F32)
    bq1 = const("bq1", [P, KT], F32)
    bq1s = const("bq1s", [P, KT], F32)
    bk1 = const("bk1", [P, KT], F32)
    bv1 = const("bv1", [P, KT], F32)
    b1_1 = const("b1_1", [P, NEXP * HB], F32)
    gw = const("gw", [P, 2, KT, NEXP], F32)
    gwh = const("gwh", [P, 2, KT, NEXP], F32R)
    gwl = const("gwl", [P, 2, KT, NEXP], F32R)
    gbias = const("gbias", [P, 2, NEXP], F32)
    eps1 = const("eps1", [P, 2], F32)
    b2 = const("b2", [NEXP, 2, D], F32)
    row0 = const("row0", [P, D], F32)
    gates = const("gates", [P, NT, NEXP], F32)
    gtmp = const("gtmp", [P, NT, NEXP], F32)
    gsum = const("gsum", [P, NT], F32)
    lower = const("lower", [P, NEXP, NEXP], F32)
    gatesT = const("gatesT", [NEXP, N], F32)
    neg_max = const("neg_max", [P, 4], F32)
    denom = const("denom", [P, 4], F32)
    rden = const("rden", [P, 4], F32)

    RAW = const("RAW", [P, 4, D], F32)
    WH = const("WH", [P, 8, D], F32R)
    WL = const("WL", [P, 8, D], F32R)
    X = const("X", [P, NT, D], F32)

    A0 = place[0]
    K = 1024

    def arena(name, shape, dt, kb):
        return nc.alloc_sbuf_tensor_at(name, shape, dt, offset=A0 + int(kb * K))

    XTH = arena("XTH", [P, KT, N], F32R, 0)
    XTL = arena("XTL", [P, KT, N], F32R, 16)
    SR = arena("SR", [P, NT, N], F32, 0)
    QH = arena("QH", [P, KT, N], F32R, 32)
    QL = arena("QL", [P, KT, N], F32R, 48)
    KH = arena("KH", [P, KT, N], F32R, 64)
    KL = arena("KL", [P, KT, N], F32R, 80)
    VH = arena("VH", [P, NT, D], F32R, 96)
    VL = arena("VL", [P, NT, D], F32R, 112)
    XN0 = arena("XN0", [P, NT, D], F32, 96)
    zeros = arena("zeros", [P, 2048], F32, 112)
    CT = arena("CT", [P, 2, TABLES, N], F32, 32)
    PR = arena("PR", [P, 2, N], F32, 64)
    PTH = arena("PTH", [P, 2, N], F32R, 72)
    PTL = arena("PTL", [P, 2, N], F32R, 80)
    src_i = arena("src_i", [P, EC], I32, 120)
    dst_i = arena("dst_i", [P, EC], I32, 121)
    junk = arena("junk", [P, 2, 4, P], F32, 122)
    src16 = arena("src16", [P, EC], F16, 128)
    dst16 = arena("dst16", [P, EC], F16, 128.5)
    key = arena("key", [P, EC], F32, 129)
    key_spare = arena("key_spare", [P, EC], F32, 130)
    multi = arena("multi", [P, EC], F32, 131)
    index = arena("index", [P, EC], U32, 132)
    count = arena("count", [P, EC], F32, 133)
    moved = arena("moved", [P, EC], F32, 134)
    XN = arena("XN", [P, NT, D], F32, 32)
    HF = arena("HF", [P, HB, N], F32, 48)
    HH = arena("HH", [P, 2, HB, N], F32R, 56)
    HL = arena("HL", [P, 2, HB, N], F32R, 72)
    cmp4 = arena("cmp4", [P, 2, NT, NEXP, NEXP], F32, 88)
    XNH = arena("XNH", [P, NT, D], F32R, 48)
    XNL = arena("XNL", [P, NT, D], F32R, 64)
    CG = arena("CG", [P, 2, N], F32, 80)
    CGH = arena("CGH", [P, 2, N], F32R, 88)
    CGL = arena("CGL", [P, 2, N], F32R, 96)
    MF = arena("MF", [P, 2, N], F32, 80)
    MH = arena("MH", [P, 4, N], F32R, 48)
    ML = arena("ML", [P, 4, N], F32R, 64)
    AQH = arena("AQH", [P, N], F32R, 48)
    AQL = arena("AQL", [P, N], F32R, 52)
    AKH = arena("AKH", [P, N], F32R, 56)
    AKL = arena("AKL", [P, N], F32R, 60)
    AVH = arena("AVH", [P, NT, 2, P], F32R, 64)
    AVL = arena("AVL", [P, NT, 2, P], F32R, 72)
    AP_ = arena("AP_", [P, 4, N], F32, 80)
    APH = arena("APH", [P, 2, NT, 2 * P], F32R, 96)
    APL = arena("APL", [P, 2, NT, 2 * P], F32R, 112)
    CXH = arena("CXH", [P, N], F32R, 128)
    CXL = arena("CXL", [P, N], F32R, 132)
    rows1 = arena("rows1", [P, 4, D], F32, 112)
    assert A0 + 136 * K <= nc.sbuf_usable_end, (A0, nc.sbuf_usable_end)

    PS = nc.alloc_psum_tensor("PS", [P, 8, 512], F32)

    def banks(b, n=2):
        return PS[:, b:b + n, :].rearrange("p a b -> p (a b)")

    tables = [nc.dram_tensor(f"edge_table{r}", (N * N + P, 1), F32, kind="Internal").ap() for r in range(TABLES)]
    counts_d = nc.dram_tensor("counts", (N, N), F32, kind="Internal").ap()

    def sem(name):
        return nc.alloc_semaphore(name)

    def f(t):
        return t.bitcast(F32)

    x_in, edges_in, cols0_in, cols_in = sem("x_in"), sem("edges_in"), sem("cols0_in"), sem("cols_in")
    row0_in, row0b_in, rows1_in = sem("row0_in"), sem("row0b_in"), sem("rows1_in")
    zeros_set, tables_clear = sem("zeros_set"), [sem(f"table{r}_clear") for r in range(TABLES)]
    setup = sem("setup")
    keys_cast, keys_dve = sem("keys_cast"), sem("keys_dve")
    keyrow_ps, keyrow_used = sem("keyrow_ps"), [sem(f"keyrow_used{i}") for i in range(2)]
    dedup_dve, edges_ready = sem("dedup_dve"), sem("edges_ready")
    staged, scattered = sem("staged"), [sem(f"scattered{r}") for r in range(TABLES)]
    raw_in = [sem(f"raw_in{s}") for s in range(4)]
    w_hi, w_ready = sem("w_hi"), sem("w_ready")
    gw_hi, gw_ready = sem("gw_hi"), sem("gw_ready")

    def stage_semaphores(stage, names, **rings):
        one = {n: sem(f"{stage}_{n}") for n in names.split()}
        more = {n: [sem(f"{stage}_{n}{i}") for i in range(k)] for n, k in rings.items()}
        return {**one, **more}

    LN = stage_semaphores("norm", "dve var root xn")
    TR = stage_semaphores("xt", "ps hi done")
    Q0 = stage_semaphores("qkv0", "ps hi v_ps v_hi v_done s_ps s_done bias", lo=2)
    A = stage_semaphores("att0", "sum1 summed penalty m1 m2 mx exp rden stored", c_in=2, t_ps=2, t_hi=2, t_lo=2, av_ps=2, done=2)
    M = stage_semaphores("moe", "lg_ps gate_dve shifted g_exp gates gt_ps gt g_ps acc h_ps hh hl y_ps", w2used=2, gelu=2, yfree=4)
    G = stage_semaphores("gnn", "hi lo eps diag chi clo ps rt_hi rt_lo h_ps mh y_ps featsum", c_in=2, relu=2, ml=2, yfree=4)
    B = stage_semaphores("att1", "bq scaled q_ps q_hi q_lo k_ps k_hi k_lo v_ps v_hi v_lo v_zero s_ps mx exp rden norm t_ps t_hi t_lo pv_ps "
              "cx_hi cx_lo y_ps bias", yfree=4)
    row0c_in = sem("row0c_in")
    F = stage_semaphores("fin", "g1 n1 g2 n2 done out")

    wq = {0: a["L0_gnn_Wq"], 1: a["L1_ffn_Wq"]}
    wk = {0: a["L0_gnn_Wk"], 1: a["L1_ffn_Wk"]}

    def colblock(w, n):
        return w.rearrange("(k p) n -> p k n", p=P)[:, :, ds(n * P, P)]

    U_FFN0 = 12
    U_GNN = U_FFN0 + 4 * NEXP
    U_ATT = U_GNN + 2 * GB
    U_MOE1 = U_ATT + 16

    def raw3(s):
        return RAW[:, s, :].rearrange("p (k n) -> p k n", k=KT)

    def wblk(t, s, k):
        return t[:, s, k * P:(k + 1) * P]

    def three_pass(pe, outs, lh, ll, rh, rl, first, last):
        for lhs, rhs, j in ((lh, rh, 0), (lh, rl, 1), (ll, rh, 2)):
            for o, r in zip(outs, rhs):
                got = pe.matmul(o, lhs, r, start=first and j == 0, stop=last and j == 2)
        return got

    def halves(t, k):
        return [t[:, k, h * HALF:(h + 1) * HALF] for h in range(2)]

    block = ctx.enter_context(nc.Block())

    @block.sync
    def _(sp):
        def wait(s, value):
            sp.wait_ge(s, value)
            if not isinstance(value, int):
                sp.nop(nofuse=True)

        def load(u, dst_ap, src_ap, s, j):
            if j is None or j >= 4:
                wait(w_ready, u - 3)
            sp.dma_start(dst_ap, src_ap).then_inc(raw_in[s], 16)

        pt = "(p c) -> p c"
        sp.dma_start(src_i[:, :], a["src"].rearrange(pt, p=P)).then_inc(edges_in, 16)
        sp.dma_start(dst_i[:, :], a["dst"].rearrange(pt, p=P)).then_inc(edges_in, 16)
        sp.dma_start(X[:, :, :], a["x"].rearrange("(t p) d -> p t d", p=P)).then_inc(x_in, 16)
        with nc.allow_non_contiguous_dma(reason="biases, one feature per partition"):
            sp.dma_start(bq0[:, :], a["L0_gnn_bq"].rearrange("(k p) -> p k", p=P)).then_inc(cols0_in, 16)
            sp.dma_start(bk0[:, :], a["L0_gnn_bk"].rearrange("(k p) -> p k", p=P)).then_inc(cols0_in, 16)
        for u in range(4):
            load(u, raw3(u), colblock((wq, wk)[u % 2][0], u // 2), u, u)
        wait(zeros_set, 1)
        for r in range(TABLES):
            sp.dma_start(tables[r][0:N * N, :].rearrange("(p c f) o -> p c (f o)", p=P, c=4),
                         zeros[:, :].unsqueeze(1).to_broadcast([P, 4, 2048])).then_inc(tables_clear[r], 16)
            sp.dma_start(tables[r][N * N:N * N + P, :], zeros[:, 0:1]).then_inc(tables_clear[r], 16)
        for u in range(4, 8):
            load(u, raw3(u % 4), colblock((wq, wk)[u % 2][0], u // 2), u % 4, u)
        for k in range(KT):
            load(8 + k, RAW[:, k, :], a["L0_gnn_Wv"][k * P:(k + 1) * P, :], k, 8 + k)
        sp.dma_start(row0[:, :], a["L0_gnn_bv"].partition_broadcast(P)).then_inc(row0_in, 16)
        with nc.allow_non_contiguous_dma(reason="biases, one feature per partition"):
            for t, n in ((gb1, "L1_gnn_b1"), (bq1, "L1_ffn_bq"), (bk1, "L1_ffn_bk"), (bv1, "L1_ffn_bv")):
                sp.dma_start(t[:, :], a[n].rearrange("(k p) -> p k", p=P)).then_inc(cols_in, 16)
            for t, n in ((b1_0, "L0_ffn_b1"), (b1_1, "L1_ffn_b1")):
                sp.dma_start(t[:, :], a[n].rearrange("e (k p) -> p (e k)", p=P)).then_inc(cols_in, 16)
            for m, n in enumerate(("L0_ffn_gate_w", "L1_ffn_Wg")):
                sp.dma_start(gw[:, m, :, :], a[n].rearrange("(k p) e -> p k e", p=P)).then_inc(cols_in, 16)
        for m, n in enumerate(("L0_ffn_gate_b", "L1_ffn_bg")):
            sp.dma_start(gbias[:, m, :], a[n].partition_broadcast(P)).then_inc(cols_in, 16)
        for m, n in enumerate(("L0_ffn_b2", "L1_ffn_b2")):
            sp.dma_start(b2[:, m, :], a[n]).then_inc(cols_in, 16)
        sp.dma_start(eps1[:, 0:1], a["L1_gnn_eps"].partition_broadcast(P)).then_inc(cols_in, 16)

        def moe_load(u0, w1, w2):
            def load_w1(e, u, s):
                for b in range(HB):
                    load(u + b, raw3((s + b) % 4),
                         w1[ds(e)].rearrange("a (k p) h -> p (a k) h", p=P)[:, :, b * P:(b + 1) * P], (s + b) % 4, None)

            def load_w2(e, u, s):
                for b in range(HB):
                    load(u + b, RAW[:, (s + b) % 4, :],
                         w2[ds(e)].rearrange("a (k p) h -> p (a k) h", p=P)[:, b, :], (s + b) % 4, None)

            if u0 != U_FFN0:
                load_w1(0, u0, 0)
            with sp.Fori(0, NEXP - 1) as m:
                load_w1(m + 1, u0 + 2 + 4 * m, 2)
                load_w2(m, u0 + 4 + 4 * m, 0)
            load_w2(NEXP - 1, u0 + 4 * NEXP - 2, 2)

        for b in range(HB):
            load(U_FFN0 + b, raw3(b), a["L0_ffn_w1"][0].rearrange("(k p) h -> p k h", p=P)[:, :, b * P:(b + 1) * P], b, None)

        for r in range(TABLES):
            wait(scattered[r], 16 * QUADS)

        def count_in(t, par):
            for r in range(TABLES):
                sp.dma_start(CT[:, par, r, :],
                             tables[r][ds(t * P * N, P * N), :].rearrange("(p f) o -> p (f o)", p=P)).then_inc(A["c_in"][par], 16)

        def count_out(t, par):
            sp.dma_start(counts_d[ds(t * P, P), :], CT[:, par, 0, :]).then_inc(A["stored"], 16)

        wait(Q0["s_done"], NT)
        count_in(0, 0)
        count_in(1, 1)
        with sp.Fori(0, NT // 2 - 1) as i:
            for par in range(2):
                wait(A["summed"], 2 * i + par + 1)
                count_out(2 * i + par, par)
                wait(A["exp"], 2 * i + par + 1)
                wait(A["stored"], 32 * i + 16 * par + 16)
                count_in(2 * i + par + 2, par)
        for t in (NT - 2, NT - 1):
            wait(A["summed"], t + 1)
            count_out(t, t % 2)
        moe_load(U_FFN0, a["L0_ffn_w1"], a["L0_ffn_w2"])

        wait(Q0["bias"], 1)
        sp.dma_start(row0[:, :], a["L1_gnn_b2"].partition_broadcast(P)).then_inc(row0b_in, 16)
        wait(A["stored"], 16 * NT)
        for par in range(2):
            wait(M["w2used"][par], NEXP // 2)

        def gcount_in(t, par):
            sp.dma_start(CG[:, par, :], counts_d[ds(t * P, P), :]).then_inc(G["c_in"][par], 16)

        gcount_in(0, 0)
        gcount_in(1, 1)
        with sp.Fori(0, NT // 2 - 1) as i:
            for par in range(2):
                wait(G["clo"], 2 * i + par + 1)
                gcount_in(2 * i + par + 2, par)
        with sp.Fori(0, 2) as g:
            for n in range(4):
                load(U_GNN + 8 * g + n, raw3(n), colblock(a["L1_gnn_W1"], 4 * g + n), n, None)
            for n in range(4):
                load(U_GNN + 8 * g + 4 + n, RAW[:, n, :], a["L1_gnn_W2"][ds((4 * g + n) * P, P), :], n, None)

        wait(G["featsum"], 1)
        sp.dma_start(row0[:, :], a["L1_ffn_bo"].partition_broadcast(P)).then_inc(row0c_in, 16)

        def qkv_in(hp, u, s):
            for j, n in enumerate(("L1_ffn_Wq", "L1_ffn_Wk", "L1_ffn_Wv")):
                load(u + j, raw3((s + j) % 4), colblock(a[n], hp), (s + j) % 4, None)

        qkv_in(0, U_ATT, 0)
        with sp.Fori(0, KT - 1) as hp:
            load(U_ATT + 3 + 4 * hp, RAW[:, 3, :], a["L1_ffn_Wo"][ds(hp * P, P), :], 3, None)
            qkv_in(hp + 1, U_ATT + 4 + 4 * hp, 0)
        load(U_ATT + 15, RAW[:, 3, :], a["L1_ffn_Wo"][(KT - 1) * P:KT * P, :], 3, None)
        wait(B["y_ps"], NT * KT)
        for j, n in enumerate(("L1_ffn_g1", "L1_ffn_beta1", "L1_ffn_g2", "L1_ffn_beta2")):
            sp.dma_start(rows1[:, j, :], a[n].partition_broadcast(P)).then_inc(rows1_in, 16)
        moe_load(U_MOE1, a["L1_ffn_W1"], a["L1_ffn_W2"])

        for t in range(NT):
            wait(F["done"], t + 1)
            sp.dma_start(out[t * P:(t + 1) * P, :], X[:, t, :]).then_inc(F["out"], 16)
        wait(F["out"], 16 * NT)

    @block.gpsimd
    def _(gp):
        def wait(s, value):
            gp.wait_ge(s, value)
            if not isinstance(value, int):
                gp.nop(nofuse=True)

        gp.memset(zeros[:, :], 0.0).then_inc(zeros_set, 1)
        gp.memset(ident[:, :], 0.0).then_inc(setup, 1)
        gp.memset(ident16[:, :], 0.0).then_inc(setup, 1)
        gp.memset(ident1024[:, :], 0.0).then_inc(setup, 1)
        gp.memset(earlier[:, :], 257.0).then_inc(setup, 1)
        gp.memset(lower[:, :, :], 1.0).then_inc(setup, 1)
        wait(setup, 5)
        for t, v in ((ident, 1.0), (ident16, 1.0), (ident1024, 1024.0)):
            gp.affine_select(out=t[:, :], in_=t[:, :], compare_op=ALU.not_equal, fill=v,
                             base=0, pattern=[[-1, P]], channel_multiplier=1).then_inc(setup, 1)
        gp.affine_select(out=earlier[:, :], in_=earlier[:, :], compare_op=ALU.is_gt, fill=1.0,
                         base=0, pattern=[[-1, P]], channel_multiplier=1).then_inc(setup, 1)
        gp.affine_select(out=lower[:, :, :], in_=lower[:, :, :], compare_op=ALU.is_gt, fill=0.0,
                         base=0, pattern=[[1, NEXP], [-1, NEXP]], channel_multiplier=0).then_inc(setup, 1)
        gp.iota(spare[:, :], pattern=[[0, 1]], base=N * N, channel_multiplier=1,
                allow_small_or_imprecise_dtypes=True).then_inc(setup, 1)

        for r in range(TABLES):
            wait(tables_clear[r], 32)
        with gp.Fori(0, QUADS // 2) as i:
            for par in range(2):
                q = 2 * i + par
                wait(edges_ready, q + 1)
                gp.tensor_copy(index_s[:, par, :], index[:, ds(4 * q, 4)]).then_inc(staged, 1)
                gp.tensor_copy(count_s[:, par, :], count[:, ds(4 * q, 4)]).then_inc(staged, 1)
                wait(staged, 2 * q + 2)
                for r in range(TABLES):
                    wait(scattered[r], 16 * q)
                    gp.indirect_dma_start(
                        out=tables[r], out_offset=bass.IndirectOffsetOnAxis(ap=index_s[:, par, r:r + 1], axis=0),
                        in_=count_s[:, par, r:r + 1], in_offset=None, compute_op=ALU.add).then_inc(scattered[r], 16)

        def split(u, turn, raw, slot, scaled=None):
            wait(raw_in[raw], 16 * (turn + 1))
            if scaled is not None:
                gp.tensor_scalar(RAW[:, raw, :], RAW[:, raw, :], DH ** -0.5, None, ALU.mult).then_inc(B["scaled"], 1)
                wait(B["scaled"], scaled + 1)
            gp.tensor_copy(WH[:, slot, :], RAW[:, raw, :]).then_inc(w_hi, 1)
            wait(w_hi, u + 1)
            gp.tensor_tensor(WL[:, slot, :], RAW[:, raw, :], f(WH[:, slot, :]), ALU.subtract).then_inc(w_ready, 1)

        wait(w_ready, U_FFN0)
        wait(Q0["ps"], 8)
        for b in range(HB):
            split(U_FFN0 + b, U_FFN0 // 4, b, b)

        with gp.Fori(0, NT // 2) as i:
            for par in range(2):
                t = 2 * i + par
                wait(A["c_in"][par], 64 * i + 64)
                gp.tensor_tensor(CT[:, par, 0, :], CT[:, par, 0, :], CT[:, par, 1, :], ALU.add).then_inc(A["sum1"], 1)
                gp.tensor_tensor(CT[:, par, 2, :], CT[:, par, 2, :], CT[:, par, 3, :], ALU.add).then_inc(A["sum1"], 1)
                wait(A["sum1"], 2 * t + 2)
                gp.tensor_tensor(CT[:, par, 0, :], CT[:, par, 0, :], CT[:, par, 2, :], ALU.add).then_inc(A["summed"], 1)
                wait(A["summed"], t + 1)
                gp.tensor_scalar(CT[:, par, 1, :], CT[:, par, 0, :], 1.0, NEG, ALU.min, ALU.mult).then_inc(A["penalty"], 1)

        def moe_split(which, u0, skip_first):
            if not skip_first:
                for b in range(HB):
                    split(u0 + b, u0 // 4, b, b)

            def pair(half, par, last=False):
                m = 2 * half + par
                if not last:
                    wait(M["h_ps"], which * (HB * NEXP) + 2 * m)
                    for b in range(HB):
                        split(u0 + 2 + 4 * m + b, u0 // 4 + m, 2 + b, 2 * (1 - par) + b)
                wait(M["w2used"][par], which * (NEXP // 2) + half)
                for b in range(HB):
                    if last:
                        split(u0 + 4 * NEXP - 2 + b, u0 // 4 + NEXP - 1, 2 + b, 4 + 2 * par + b)
                    else:
                        split(u0 + 4 + 4 * m + b, u0 // 4 + 1 + m, b, 4 + 2 * par + b)

            with gp.Fori(0, NEXP // 2 - 1) as i:
                pair(i, 0)
                pair(i, 1)
            pair(NEXP // 2 - 1, 0)
            pair(NEXP // 2 - 1, 1, last=True)

        wait(Q0["v_ps"], NT)
        moe_split(0, U_FFN0, True)

        wait(M["h_ps"], 2 * NEXP)
        for par in range(2):
            wait(M["w2used"][par], NEXP // 2)
        with gp.Fori(0, 2) as g:
            wait(G["h_ps"], 4 * g)
            for n in range(4):
                split(U_GNN + 8 * g + n, U_GNN // 4 + 2 * g, n, n)
            wait(G["y_ps"], NT * g)
            for n in range(4):
                split(U_GNN + 8 * g + 4 + n, U_GNN // 4 + 2 * g + 1, n, 4 + n)

        wait(G["y_ps"], 2 * NT)
        gp.memset(f(AVH[:, :, :, :]), 0.0).then_inc(B["v_zero"], 1)
        gp.memset(f(AVL[:, :, :, :]), 0.0).then_inc(B["v_zero"], 1)

        def qkv_split(hp, j):
            if j == 0:
                wait(B["q_ps"], hp)
            elif j == 1:
                wait(B["k_ps"], hp)
            else:
                wait(B["v_ps"], hp)
            split(U_ATT + 4 * hp + j, U_ATT // 4 + hp, j, j, scaled=hp if j == 0 else None)

        def heads(hp, last):
            for m in range(2 * NT):
                wait(B["rden"], 2 * NT * hp + m + 1)
                gp.tensor_scalar(AP_[:, m % 4, :], AP_[:, m % 4, :], rden[:, m % 4:m % 4 + 1], None,
                                 ALU.mult).then_inc(B["norm"], 1)
                if m == 6:
                    wait(B["y_ps"], NT * hp)
                    split(U_ATT + 4 * hp + 3, U_ATT // 4 + hp, 3, 3)
                if m in (8, 10, 12) and not last:
                    qkv_split(hp + 1, (m - 8) // 2)

        for j in range(3):
            qkv_split(0, j)
        with gp.Fori(0, KT - 1) as hp:
            heads(hp, False)
        heads(KT - 1, True)

        wait(B["y_ps"], NT * KT)
        moe_split(1, U_MOE1, False)

    @block.scalar
    def _(act):
        def wait(s, value):
            act.wait_ge(s, value)
            if not isinstance(value, int):
                act.nop(nofuse=True)

        def copy(dst, src, s, **kw):
            act.activation(dst, src, Copy, **kw).then_inc(s, 1)

        def root(turn):
            act.wait_ge(LN["var"], turn + 1)
            act.activation(rstd[:, :], ve[:, :], ACT.Sqrt).then_inc(LN["root"], 1)

        def transposed(turn):
            for t in range(NT):
                act.wait_ge(TR["ps"], NT * turn + t + 1)
                copy(XTH[:, :, t * P:(t + 1) * P], PS[:, t % 2, :].rearrange("p (k n) -> p k n", k=KT), TR["hi"])

        def w_hi_of(u, turn, raw, slot):
            act.wait_ge(raw_in[raw], 16 * (turn + 1))
            copy(WH[:, slot, :], RAW[:, raw, :], w_hi)

        root(0)
        for u in range(4):
            w_hi_of(u, 0, u, u)
        transposed(0)
        act.wait_ge(cols0_in, 32)
        with act.Fori(0, 2) as i:
            for j in range(4):
                n = 2 * i + j // 2
                dst, bias = ((QH, bq0), (KH, bk0))[j % 2]
                wait(Q0["ps"], 4 * i + j + 1)
                act.activation(dst[:, ds(n), :].rearrange("p a n -> p (a n)"), banks(2 * (j % 2)), Identity,
                               bias=bias[:, ds(n)]).then_inc(Q0["hi"], 1)
                act.wait_ge(raw_in[j], 16 * i + 32)
                copy(WH[:, ds(4 * i + j), :].rearrange("p a n -> p (a n)"), RAW[:, j, :], w_hi)
        for t in range(NT):
            act.wait_ge(Q0["v_ps"], t + 1)
            copy(VH[:, t, :], PS[:, t % 4, :], Q0["v_hi"])
        for t in range(NT):
            act.wait_ge(Q0["s_ps"], t + 1)
            copy(SR[:, t, :], banks(4 + 2 * (t % 2)), Q0["s_done"], scale=D ** -0.5)

        def softmax(half, par):
            t = 2 * half + par
            act.wait_ge(A["mx"], t + 1)
            act.wait_ge(A["t_ps"][par], half)
            act.activation(PR[:, par, :], CT[:, par, 3, :], ACT.Exp, bias=neg_max[:, par:par + 1],
                           accum_out=denom[:, par:par + 1]).then_inc(A["exp"], 1)

        def p_hi(half, par):
            act.wait_ge(A["t_ps"][par], half + 1)
            act.wait_ge(A["av_ps"][par], half)
            copy(PTH[:, par, :], banks(4 + 2 * par), A["t_hi"][par])

        softmax(0, 0)
        softmax(0, 1)
        p_hi(0, 0)
        with act.Fori(0, NT // 2 - 1) as i:
            softmax(i + 1, 0)
            p_hi(i, 1)
            softmax(i + 1, 1)
            p_hi(i + 1, 0)
        p_hi(NT // 2 - 1, 1)

        def moe(turn, which):
            transposed(turn)
            if which == 0:
                act.wait_ge(cols_in, 16 * 13)
                copy(gwh[:, :, :, :], gw[:, :, :, :], gw_hi)
                act.wait_ge(M["shifted"], 1)
                act.activation(gtmp[:, :, :], gtmp[:, :, :], ACT.Exp).then_inc(M["g_exp"], 1)
            b1 = (b1_0, b1_1)[which]

            def hidden(half, par):
                e = 2 * half + par
                for b in range(HB):
                    act.wait_ge(M["h_ps"], which * (HB * NEXP) + 2 * e + b + 1)
                    wait(M["hl"], which * (HB * NEXP) + 2 * e)
                    act.activation(HF[:, b, :], banks(2 * b), ACT.Gelu,
                                   bias=b1[:, ds(2 * e + b)]).then_inc(M["gelu"][b], 1)
                    act.wait_ge(M["gelu"][b], which * NEXP + e + 1)
                    act.wait_ge(M["w2used"][par], which * (NEXP // 2) + half)
                    copy(HH[:, par, b, :], HF[:, b, :], M["hh"])

            def transposed_gates():
                act.wait_ge(M["gt_ps"], which + 1)
                copy(gatesT[:, :], PS[0:NEXP, 4:6, :].rearrange("p a b -> p (a b)"), M["gt"])

            hidden(0, 0)
            transposed_gates()
            with act.Fori(0, NEXP // 2 - 1) as i:
                hidden(i, 1)
                hidden(i + 1, 0)
            hidden(NEXP // 2 - 1, 1)

        root(1)
        moe(1, 0)

        root(2)
        for t in range(NT):
            act.wait_ge(LN["xn"], NT * 2 + t + 1)
            copy(XNH[:, t, :], XN[:, t, :], G["hi"])
        for t in range(NT):
            act.wait_ge(G["diag"], t + 1)
            if t >= 2:
                act.wait_ge(G["ps"], t - 1)
            copy(CGH[:, t % 2, :], CG[:, t % 2, :], G["chi"])
        act.wait_ge(G["ps"], NT)
        for k in range(KT):
            copy(XTH[:, k, :], banks(2 * k), G["rt_hi"])
        with act.Fori(0, 2) as g:
            for n in range(4):
                act.wait_ge(G["h_ps"], 4 * g + n + 1)
                wait(G["ml"][n % 2], 2 * g + n // 2)
                act.activation(MF[:, n % 2, :], banks(2 * (n % 2)), ACT.Relu,
                               bias=gb1[:, ds(4 * g + n)]).then_inc(G["relu"][n % 2], 1)
                act.wait_ge(G["relu"][n % 2], 2 * g + n // 2 + 1)
                copy(MH[:, n, :], MF[:, n % 2, :], G["mh"])

        root(3)
        transposed(2)
        act.wait_ge(B["v_zero"], 2)
        act.wait_ge(B["bq"], 1)

        def heads(hp):
            wait(B["q_ps"], hp + 1)
            act.activation(AQH[:, :], banks(0), Identity, bias=bq1s[:, ds(hp)]).then_inc(B["q_hi"], 1)
            wait(B["k_ps"], hp + 1)
            act.activation(AKH[:, :], banks(2), Identity, bias=bk1[:, ds(hp)]).then_inc(B["k_hi"], 1)
            act.wait_ge(B["v_ps"], hp + 1)
            for h in range(2):
                c = slice(h * DH, (h + 1) * DH)
                copy(AVH[:, :, h, c], banks(4).rearrange("p (t c) -> p t c", t=NT)[:, :, c], B["v_hi"])

            def softmax(m):
                act.wait_ge(B["mx"], 2 * NT * hp + m + 1)
                if m >= 4:
                    act.wait_ge(B["t_ps"], 2 * NT * hp + m - 3)
                act.activation(AP_[:, m % 4, :], banks(2 * (m % 2)), ACT.Exp, bias=neg_max[:, m % 4:m % 4 + 1],
                               accum_out=denom[:, m % 4:m % 4 + 1]).then_inc(B["exp"], 1)

            def context(qp):
                wait(B["pv_ps"], 8 * hp + 2 * qp + 2)
                act.activation(CXH[:, 2 * P * qp:2 * P * (qp + 1)], PS[:, 6 + qp % 2, 0:2 * P], Identity,
                               bias=bv1[:, ds(hp)]).then_inc(B["cx_hi"], 1)

            softmax(0)
            softmax(1)
            for m in range(2 * NT):
                g = m // 2
                act.wait_ge(B["t_ps"], 2 * NT * hp + m + 1)
                if g >= 2:
                    act.wait_ge(B["pv_ps"], 8 * hp + g - 1)
                copy(APH[:, g % 2, :, (m % 2) * P:(m % 2 + 1) * P], banks(4).rearrange("p (k q) -> p k q", k=NT), B["t_hi"])
                if m + 2 < 2 * NT:
                    softmax(m + 2)
                if m % 4 == 1 and m >= 5:
                    context((m - 5) // 4)
            context(3)

        with act.Fori(0, KT) as hp:
            heads(hp)

        root(4)
        moe(3, 1)
        root(5)

    @block.vector
    def _(v):
        def lo(dst, src, hi, s):
            v.tensor_tensor(dst, src, f(hi), ALU.subtract).then_inc(s, 1)

        def lo_biased(dst, src, bias, hi, s):
            v.scalar_tensor_tensor(out=dst, in0=src, scalar=bias, in1=f(hi), op0=ALU.add, op1=ALU.subtract).then_inc(s, 1)

        def layernorm(turn, src, dst):
            done = [turn * (2 * NT + 5)]

            def step(ins):
                ins.then_inc(LN["dve"], 1)
                done[0] += 1

            for t in range(NT):
                step(v.bn_stats(stats[:, t, :], src[:, t, :]))
            for t in range(NT):
                v.wait_ge(LN["dve"], turn * (2 * NT + 5) + t + 1)
                step(v.bn_aggr(mv[:, t, :], stats[:, t, :]))
            v.wait_ge(LN["dve"], done[0])
            v.tensor_scalar(ve[:, :], mv[:, :, 1], 1e-5, None, ALU.add).then_inc(LN["var"], 1)
            v.wait_ge(LN["root"], turn + 1)
            step(v.reciprocal(inv[:, :], rstd[:, :]))
            v.wait_ge(LN["dve"], done[0])
            step(v.tensor_tensor(sq[:, :], inv[:, :], inv[:, :], ALU.mult))
            v.wait_ge(LN["dve"], done[0])
            step(v.tensor_tensor(ve[:, :], sq[:, :], ve[:, :], ALU.mult))
            v.wait_ge(LN["dve"], done[0])
            step(v.tensor_scalar(ve[:, :], ve[:, :], -0.5, 1.5, ALU.mult, ALU.add))
            v.wait_ge(LN["dve"], done[0])
            step(v.tensor_tensor(rstd[:, :], inv[:, :], ve[:, :], ALU.mult))
            v.wait_ge(LN["dve"], done[0])
            for t in range(NT):
                v.tensor_scalar(dst[:, t, :], src[:, t, :], mv[:, t, 0:1], rstd[:, t:t + 1],
                                ALU.subtract, ALU.mult).then_inc(LN["xn"], 1)

        def transposed(turn):
            for t in range(NT):
                v.wait_ge(TR["hi"], NT * turn + t + 1)
                lo(XTL[:, :, t * P:(t + 1) * P], PS[:, t % 2, :].rearrange("p (k n) -> p k n", k=KT),
                   XTH[:, :, t * P:(t + 1) * P], TR["done"])

        v.wait_ge(edges_in, 32)
        v.tensor_copy(src16[:, :], src_i[:, :]).then_inc(keys_cast, 1)
        v.tensor_copy(dst16[:, :], dst_i[:, :]).then_inc(keys_cast, 1)
        v.wait_ge(keys_cast, 2)
        v.scalar_tensor_tensor(out=key[:, :], in0=src16[:, :], scalar=float(N), in1=dst16[:, :],
                               op0=ALU.mult, op1=ALU.add).then_inc(keys_dve, 1)
        v.wait_ge(keys_dve, 1)
        v.wait_ge(setup, 11)
        v.tensor_scalar(key_spare[:, :], key[:, :], spare[:, 0:1], None, ALU.subtract).then_inc(keys_dve, 1)
        v.wait_ge(keys_dve, 2)

        def quad(q, par, turn):
            v.wait_ge(keyrow_used[par], turn)
            v.wait_ge(keyrow_ps, q + 1)
            for c in range(4):
                got = v.scalar_tensor_tensor(out=junk[:, par, c, :], in0=PS[:, 6 + par, c * P:(c + 1) * P],
                                             scalar=key[:, ds(4 * q + c)], in1=earlier[:, :],
                                             op0=ALU.is_equal, op1=ALU.mult, accum_out=multi[:, ds(4 * q + c)])
            got.then_inc(keyrow_used[par], 1)

        def leaders(q, n, chunk, waits):
            for par, w in waits:
                v.wait_ge(keyrow_used[par], w)
            c = ds(4 * q, 4 * n)
            v.scalar_tensor_tensor(out=count[:, c], in0=multi[:, c], scalar=256.0, in1=multi[:, c],
                                   op0=ALU.is_lt, op1=ALU.mult).then_inc(dedup_dve, 1)
            v.scalar_tensor_tensor(out=moved[:, c], in0=multi[:, c], scalar=256.0, in1=key_spare[:, c],
                                   op0=ALU.is_lt, op1=ALU.mult).then_inc(dedup_dve, 1)
            v.wait_ge(dedup_dve, 2 * chunk + 2)
            v.tensor_scalar(index[:, c], moved[:, c], spare[:, 0:1], None, ALU.add).then_inc(edges_ready, n)

        with v.Fori(0, 5) as i:
            quad(2 * i, 0, i)
            quad(2 * i + 1, 1, i)
            leaders(2 * i, 2, i, ((0, i + 1), (1, i + 1)))

        v.wait_ge(x_in, 16)
        layernorm(0, X, XN0)
        for u in range(4):
            v.wait_ge(w_hi, u + 1)
            lo(WL[:, u, :], RAW[:, u, :], WH[:, u, :], w_ready)
        transposed(0)
        with v.Fori(0, 2) as i:
            for j in range(4):
                n = 2 * i + j // 2
                first = 10 + 12 * i + 3 * j
                for c in range(3):
                    quad(first + c, (3 * j + c) % 2, 5 + 6 * i + (3 * j + c) // 2)
                leaders(first, 3, 5 + 4 * i + j, [(p, 6 * i + 5 + (3 * j + 3 + 1 - p) // 2) for p in range(2)])
                dst, hi_, bias = ((QL, QH, bq0), (KL, KH, bk0))[j % 2]
                v.wait_ge(Q0["hi"], 4 * i + j + 1)
                lo_biased(dst[:, ds(n), :].rearrange("p a n -> p (a n)"), banks(2 * (j % 2)), bias[:, ds(n)],
                          hi_[:, ds(n), :].rearrange("p a n -> p (a n)"), Q0["lo"][j % 2])
                v.wait_ge(w_hi, 4 * i + j + 5)
                lo(WL[:, ds(4 * i + j), :].rearrange("p a n -> p (a n)"), RAW[:, j, :],
                   WH[:, ds(4 * i + j), :].rearrange("p a n -> p (a n)"), w_ready)
        for r in range(TABLES):
            v.wait_ge(tables_clear[r], 32)
        for t in range(NT):
            v.wait_ge(Q0["v_hi"], t + 1)
            lo(VL[:, t, :], PS[:, t % 4, :], VH[:, t, :], Q0["v_done"])
        v.wait_ge(row0_in, 16)
        v.tensor_tensor(X[:, :, :], X[:, :, :], row0[:, :].unsqueeze(1).to_broadcast([P, NT, D]), ALU.add).then_inc(Q0["bias"], 1)
        v.wait_ge(Q0["bias"], 1)

        def mask(half, par):
            t = 2 * half + par
            v.wait_ge(A["summed"], t + 1)
            v.wait_ge(Q0["s_done"], NT)
            v.scalar_tensor_tensor(out=CT[:, par, 2, :], in0=CT[:, par, 0, :], scalar=1.0,
                                   in1=SR[:, ds(t), :].rearrange("p a n -> p (a n)"),
                                   op0=ALU.min, op1=ALU.mult).then_inc(A["m1"], 1)
            v.wait_ge(A["m1"], t + 1)
            v.wait_ge(A["penalty"], t + 1)
            v.scalar_tensor_tensor(out=CT[:, par, 3, :], in0=CT[:, par, 1, :], scalar=NEG, in1=CT[:, par, 2, :],
                                   op0=ALU.subtract, op1=ALU.add).then_inc(A["m2"], 1)
            v.wait_ge(A["m2"], t + 1)
            v.tensor_reduce(out=neg_max[:, par:par + 1], in_=CT[:, par, 3, :], axis=X_AXIS, op=ALU.max,
                            negate=True).then_inc(A["mx"], 1)

        def p_lo(half, par):
            v.wait_ge(A["done"][par], half)
            v.wait_ge(A["exp"], 2 * half + par + 1)
            v.reciprocal(rden[:, par:par + 1], denom[:, par:par + 1]).then_inc(A["rden"], 1)
            v.wait_ge(A["t_hi"][par], half + 1)
            lo(PTL[:, par, :], banks(4 + 2 * par), PTH[:, par, :], A["t_lo"][par])

        def residual(half, par):
            t = 2 * half + par
            v.wait_ge(A["av_ps"][par], half + 1)
            v.wait_ge(A["rden"], t + 1)
            x = X[:, ds(t), :].rearrange("p a n -> p (a n)")
            v.scalar_tensor_tensor(out=x, in0=PS[:, par, :], scalar=rden[:, par:par + 1], in1=x,
                                   op0=ALU.mult, op1=ALU.add).then_inc(A["done"][par], 1)

        mask(0, 0)
        mask(0, 1)
        p_lo(0, 0)
        with v.Fori(0, NT // 2 - 1) as i:
            mask(i + 1, 0)
            p_lo(i, 1)
            residual(i, 0)
            mask(i + 1, 1)
            p_lo(i + 1, 0)
            residual(i, 1)
        p_lo(NT // 2 - 1, 1)
        residual(NT // 2 - 1, 0)
        residual(NT // 2 - 1, 1)
        v.wait_ge(A["done"][0], NT // 2)
        v.wait_ge(A["done"][1], NT // 2)

        def moe(turn, which, acc):
            transposed(turn)
            if which == 0:
                v.wait_ge(gw_hi, 1)
                lo(gwl[:, :, :, :], gw[:, :, :, :], gwh[:, :, :, :], gw_ready)
            v.wait_ge(M["lg_ps"], which * NT + NT)
            steps = [10 * which]

            def own(ins):
                ins.then_inc(M["gate_dve"], 1)
                steps[0] += 1

            own(v.tensor_tensor(gtmp[:, :, :], PS[:, 7, 0:NT * NEXP].rearrange("p (t e) -> p t e", t=NT),
                            gbias[:, which, :].unsqueeze(1).to_broadcast([P, NT, NEXP]), ALU.add))
            v.wait_ge(M["gate_dve"], steps[0])

            def wide(t):
                return t.unsqueeze(2).to_broadcast([P, NT, NEXP])

            if which == 0:
                own(v.tensor_reduce(out=gsum[:, :], in_=gtmp[:, :, :], axis=X_AXIS, op=ALU.max))
                v.wait_ge(M["gate_dve"], steps[0])
                v.tensor_tensor(gtmp[:, :, :], gtmp[:, :, :], wide(gsum[:, :]), ALU.subtract).then_inc(M["shifted"], 1)
                v.wait_ge(M["g_exp"], 1)
                own(v.tensor_reduce(out=gsum[:, :], in_=gtmp[:, :, :], axis=X_AXIS, op=ALU.add))
                v.wait_ge(M["gate_dve"], steps[0])
                own(v.reciprocal(gsum[:, :], gsum[:, :]))
                v.wait_ge(M["gate_dve"], steps[0])
                own(v.tensor_tensor(gtmp[:, :, :], gtmp[:, :, :], wide(gsum[:, :]), ALU.mult))
                v.wait_ge(M["gate_dve"], steps[0])
            shape = [P, NT, NEXP, NEXP]
            mine = gtmp[:, :, :].unsqueeze(3).to_broadcast(shape)
            other = gtmp[:, :, :].unsqueeze(2).to_broadcast(shape)
            own(v.tensor_tensor(cmp4[:, 0], other, mine, ALU.is_gt))
            own(v.tensor_tensor(cmp4[:, 1], other, mine, ALU.is_equal))
            v.wait_ge(M["gate_dve"], steps[0])
            own(v.tensor_tensor(cmp4[:, 1], cmp4[:, 1], lower[:, :, :].unsqueeze(1).to_broadcast(shape), ALU.mult))
            v.wait_ge(M["gate_dve"], steps[0])
            own(v.tensor_tensor(cmp4[:, 0], cmp4[:, 0], cmp4[:, 1], ALU.add))
            v.wait_ge(M["gate_dve"], steps[0])
            own(v.tensor_reduce(out=gates[:, :, :], in_=cmp4[:, 0], axis=X_AXIS, op=ALU.add))
            v.wait_ge(M["gate_dve"], steps[0])
            if which == 0:
                v.scalar_tensor_tensor(out=gates[:, :, :], in0=gates[:, :, :], scalar=2.0, in1=gtmp[:, :, :],
                                       op0=ALU.is_lt, op1=ALU.mult).then_inc(M["gates"], 1)
            else:
                v.tensor_scalar(gates[:, :, :], gates[:, :, :], 1.0, None, ALU.is_lt).then_inc(M["gates"], 1)

            def hidden(half, par):
                e = 2 * half + par
                for b in range(HB):
                    v.wait_ge(M["hh"], which * (HB * NEXP) + 2 * e + b + 1)
                    lo(HL[:, par, b, :], HF[:, b, :], HH[:, par, b, :], M["hl"])

            def outputs(half, par):
                m = 2 * half + par
                for t in range(NT):
                    if t < NT - 1:
                        v.wait_ge(M["y_ps"], which * ((NT - 1) * NEXP) + (NT - 1) * m + t + 1)
                    else:
                        v.wait_ge(M["w2used"][par], which * (NEXP // 2) + half + 1)
                    v.scalar_tensor_tensor(out=acc[:, t, :], in0=PS[:, 4 + t % 4, :], scalar=gates[:, t, ds(m)],
                                           in1=acc[:, t, :], op0=ALU.mult, op1=ALU.add).then_inc(M["yfree"][t % 4], 1)

            v.wait_ge(M["gates"], which + 1)
            hidden(0, 0)
            for t in range(NT):
                v.wait_ge(M["g_ps"], which * NT + t + 1)
                v.tensor_tensor(acc[:, t, :], acc[:, t, :], PS[:, 4 + t % 4, :], ALU.add).then_inc(M["acc"], 1)
            v.wait_ge(M["acc"], which * NT + NT)
            with v.Fori(0, NEXP // 2 - 1) as i:
                hidden(i, 1)
                outputs(i, 0)
                hidden(i + 1, 0)
                outputs(i, 1)
            hidden(NEXP // 2 - 1, 1)
            outputs(NEXP // 2 - 1, 0)
            outputs(NEXP // 2 - 1, 1)
            for b in range(4):
                v.wait_ge(M["yfree"][b], which * (2 * NEXP) + 2 * NEXP)

        v.wait_ge(A["stored"], 16 * NT)
        layernorm(1, X, XN)
        moe(1, 0, X)

        layernorm(2, X, XN)
        v.wait_ge(cols_in, 16 * 13)
        v.tensor_scalar(eps1[:, 1:2], eps1[:, 0:1], 1.0, None, ALU.add).then_inc(G["eps"], 1)
        v.wait_ge(G["eps"], 1)

        def diagonal(t):
            v.wait_ge(G["c_in"][t % 2], 16 * (t // 2) + 16)
            c = CG[:, t % 2, t * P:(t + 1) * P]
            v.scalar_tensor_tensor(out=c, in0=ident[:, :], scalar=eps1[:, 1:2], in1=c,
                                   op0=ALU.mult, op1=ALU.add).then_inc(G["diag"], 1)

        for t in range(NT):
            v.wait_ge(G["hi"], t + 1)
            lo(XNL[:, t, :], XN[:, t, :], XNH[:, t, :], G["lo"])
        diagonal(0)
        for t in range(NT):
            if t + 1 < NT:
                diagonal(t + 1)
            v.wait_ge(G["chi"], t + 1)
            lo(CGL[:, t % 2, :], CG[:, t % 2, :], CGH[:, t % 2, :], G["clo"])
        v.wait_ge(row0b_in, 16)
        v.tensor_tensor(XN[:, :, :], XN[:, :, :], row0[:, :].unsqueeze(1).to_broadcast([P, NT, D]), ALU.add).then_inc(G["featsum"], 1)
        v.wait_ge(G["featsum"], 1)
        v.tensor_tensor(X[:, :, :], X[:, :, :], XN[:, :, :], ALU.add).then_inc(G["featsum"], 1)
        for k in range(KT):
            v.wait_ge(G["rt_hi"], k + 1)
            lo(XTL[:, k, :], banks(2 * k), XTH[:, k, :], G["rt_lo"])
        v.wait_ge(G["featsum"], 2)
        with v.Fori(0, 2) as g:
            for n in range(4):
                v.wait_ge(G["mh"], 4 * g + n + 1)
                lo(ML[:, n, :], MF[:, n % 2, :], MH[:, n, :], G["ml"][n % 2])
            for t in range(NT):
                v.wait_ge(G["y_ps"], NT * g + t + 1)
                v.tensor_tensor(X[:, t, :], X[:, t, :], PS[:, 4 + t % 4, :], ALU.add).then_inc(G["yfree"][t % 4], 1)
        for b in range(4):
            v.wait_ge(G["yfree"][b], 4)

        layernorm(3, X, XN)
        v.tensor_scalar(bq1s[:, :], bq1[:, :], DH ** -0.5, None, ALU.mult).then_inc(B["bq"], 1)
        transposed(2)
        v.wait_ge(row0c_in, 16)
        v.tensor_tensor(XN[:, :, :], XN[:, :, :], row0[:, :].unsqueeze(1).to_broadcast([P, NT, D]), ALU.add).then_inc(B["bias"], 1)
        v.wait_ge(B["bias"], 1)
        v.wait_ge(B["bq"], 1)
        v.wait_ge(B["v_zero"], 2)

        def heads(hp):
            v.wait_ge(B["q_hi"], hp + 1)
            lo_biased(AQL[:, :], banks(0), bq1s[:, ds(hp)], AQH[:, :], B["q_lo"])
            v.wait_ge(B["k_hi"], hp + 1)
            lo_biased(AKL[:, :], banks(2), bk1[:, ds(hp)], AKH[:, :], B["k_lo"])
            v.wait_ge(B["v_hi"], 2 * hp + 2)
            for h in range(2):
                c = slice(h * DH, (h + 1) * DH)
                lo(AVL[:, :, h, c], banks(4).rearrange("p (t c) -> p t c", t=NT)[:, :, c], AVH[:, :, h, c], B["v_lo"])

            def maximum(m):
                v.wait_ge(B["s_ps"], 2 * NT * hp + m + 1)
                v.tensor_reduce(out=neg_max[:, m % 4:m % 4 + 1], in_=banks(2 * (m % 2)), axis=X_AXIS, op=ALU.max,
                                negate=True).then_inc(B["mx"], 1)

            def inverse_sum(m):
                v.wait_ge(B["exp"], 2 * NT * hp + m + 1)
                v.reciprocal(rden[:, m % 4:m % 4 + 1], denom[:, m % 4:m % 4 + 1]).then_inc(B["rden"], 1)

            def context(qp):
                v.wait_ge(B["cx_hi"], 4 * hp + qp + 1)
                q = slice(2 * P * qp, 2 * P * (qp + 1))
                lo_biased(CXL[:, q], PS[:, 6 + qp % 2, 0:2 * P], bv1[:, ds(hp)], CXH[:, q], B["cx_lo"])

            maximum(0)
            maximum(1)
            inverse_sum(0)
            for m in range(2 * NT):
                if m + 1 < 2 * NT:
                    inverse_sum(m + 1)
                v.wait_ge(B["t_hi"], 2 * NT * hp + m + 1)
                lo(APL[:, (m // 2) % 2, :, (m % 2) * P:(m % 2 + 1) * P], banks(4).rearrange("p (k q) -> p k q", k=NT),
                   APH[:, (m // 2) % 2, :, (m % 2) * P:(m % 2 + 1) * P], B["t_lo"])
                if m + 2 < 2 * NT:
                    maximum(m + 2)
                if m % 4 == 1 and m >= 5:
                    context((m - 5) // 4)
            context(3)
            for t in range(NT):
                v.wait_ge(B["y_ps"], NT * hp + t + 1)
                v.tensor_tensor(XN[:, t, :], XN[:, t, :], PS[:, t % 4, :], ALU.add).then_inc(B["yfree"][t % 4], 1)

        with v.Fori(0, KT) as hp:
            heads(hp)
        for b in range(4):
            v.wait_ge(B["yfree"][b], 2 * KT)

        def gain(g, b, g_done, b_done):
            for t in range(NT):
                v.tensor_tensor(XN[:, t, :], XN[:, t, :], rows1[:, g, :], ALU.mult).then_inc(g_done, 1)
            for t in range(NT):
                v.wait_ge(g_done, t + 1)
                v.tensor_tensor(XN[:, t, :], XN[:, t, :], rows1[:, b, :], ALU.add).then_inc(b_done, 1)

        layernorm(4, XN, XN)
        v.wait_ge(rows1_in, 64)
        v.wait_ge(LN["xn"], NT * 5)
        gain(0, 1, F["g1"], F["n1"])
        moe(3, 1, XN)
        layernorm(5, XN, XN)
        v.wait_ge(LN["xn"], NT * 6)
        gain(2, 3, F["g2"], F["n2"])
        for t in range(NT):
            v.wait_ge(F["n2"], t + 1)
            v.tensor_tensor(X[:, t, :], X[:, t, :], XN[:, t, :], ALU.add).then_inc(F["done"], 1)

    @block.tensor
    def _(pe):
        def transposes(turn, src, ready, before):
            for t in range(NT):
                pe.wait_ge(ready, before + t + 1)
                if t >= 2:
                    pe.wait_ge(TR["done"], NT * turn + t - 1)
                for k in range(KT):
                    got = pe.transpose(PS[:, t % 2, k * P:(k + 1) * P], src[:, t, k * P:(k + 1) * P], ident[:, :])
                got.then_inc(TR["ps"], 1)

        def two_banks(b):
            return [PS[:, b, :], PS[:, b + 1, :]]

        def columns(b, slot, th=XTH, tl=XTL):
            for k in range(KT):
                got = three_pass(pe, two_banks(b), wblk(WH, slot, k), wblk(WL, slot, k), halves(th, k), halves(tl, k),
                                 k == 0, k == KT - 1)
            return got

        pe.wait_ge(setup, 11)
        pe.wait_ge(keys_cast, 2)

        def quad(q, par, turn):
            pe.wait_ge(keyrow_used[par], turn)
            for c in range(4):
                o = PS[:, 6 + par, c * P:(c + 1) * P]
                pe.matmul(o, src16[:, ds(4 * q + c)].to_broadcast([P, P]), ident1024[:, :], start=True, stop=False)
                got = pe.matmul(o, dst16[:, ds(4 * q + c)].to_broadcast([P, P]), ident16[:, :], start=False, stop=True)
            got.then_inc(keyrow_ps, 1)

        with pe.Fori(0, 5) as i:
            quad(2 * i, 0, i)
            quad(2 * i + 1, 1, i)

        transposes(0, XN0, LN["xn"], 0)
        pe.wait_ge(TR["done"], NT * 1)
        with pe.Fori(0, 2) as i:
            for j in range(4):
                for c in range(3):
                    quad(10 + 12 * i + 3 * j + c, (3 * j + c) % 2, 5 + 6 * i + (3 * j + c) // 2)
                pe.wait_ge(w_ready, 4 * i + j + 1)
                pe.wait_ge(Q0["lo"][j % 2], 2 * i + j // 2)
                columns(2 * (j % 2), j).then_inc(Q0["ps"], 1)
        pe.wait_ge(w_ready, 12)
        for par in range(2):
            pe.wait_ge(Q0["lo"][par], 4)
        for t in range(NT):
            if t >= 4:
                pe.wait_ge(Q0["v_done"], t - 3)
            q = slice(t * P, (t + 1) * P)
            for k in range(KT):
                got = three_pass(pe, [PS[:, t % 4, :]], XTH[:, k, q], XTL[:, k, q], [WH[:, 4 + k, :]], [WL[:, 4 + k, :]],
                                 k == 0, k == KT - 1)
            got.then_inc(Q0["v_ps"], 1)
        for par in range(2):
            pe.wait_ge(keyrow_used[par], QUADS // 2)
        for t in range(NT):
            if t >= 2:
                pe.wait_ge(Q0["s_done"], t - 1)
            q = slice(t * P, (t + 1) * P)
            for k in range(KT):
                got = three_pass(pe, two_banks(4 + 2 * (t % 2)), QH[:, k, q], QL[:, k, q], halves(KH, k), halves(KL, k),
                                 k == 0, k == KT - 1)
            got.then_inc(Q0["s_ps"], 1)

        def p_transposes(half, par):
            pe.wait_ge(A["exp"], 2 * half + par + 1)
            pe.wait_ge(A["t_lo"][par], half)
            for k in range(NT):
                got = pe.transpose(banks(4 + 2 * par)[:, k * P:(k + 1) * P], PR[:, par, k * P:(k + 1) * P], ident[:, :])
            got.then_inc(A["t_ps"][par], 1)

        def values(half, par):
            pe.wait_ge(A["t_lo"][par], half + 1)
            pe.wait_ge(A["done"][par], half)
            for k in range(NT):
                got = three_pass(pe, [PS[:, par, :]], PTH[:, par, k * P:(k + 1) * P], PTL[:, par, k * P:(k + 1) * P],
                                 [VH[:, k, :]], [VL[:, k, :]], k == 0, k == NT - 1)
            got.then_inc(A["av_ps"][par], 1)

        pe.wait_ge(Q0["s_done"], NT)
        pe.wait_ge(Q0["v_done"], NT)
        p_transposes(0, 0)
        with pe.Fori(0, NT // 2 - 1) as i:
            p_transposes(i, 1)
            values(i, 0)
            p_transposes(i + 1, 0)
            values(i, 1)
        p_transposes(NT // 2 - 1, 1)
        values(NT // 2 - 1, 0)
        values(NT // 2 - 1, 1)

        def moe(turn, which, ready, before, u0):
            transposes(turn, XN, ready, before)
            pe.wait_ge(TR["done"], NT * (turn + 1))
            if which == 0:
                pe.wait_ge(gw_ready, 1)
            for t in range(NT):
                q = slice(t * P, (t + 1) * P)
                for k in range(KT):
                    got = three_pass(pe, [PS[:, 7, t * NEXP:(t + 1) * NEXP]], XTH[:, k, q], XTL[:, k, q],
                                     [gwh[:, which, k, :]], [gwl[:, which, k, :]], k == 0, k == KT - 1)
                got.then_inc(M["lg_ps"], 1)

            def hidden(half, par, first=False):
                e = 2 * half + par
                for b in range(HB):
                    pe.wait_ge(w_ready, u0 + 1 + b if first else u0 + 4 * e - 1 + b)
                    pe.wait_ge(M["gelu"][b], which * NEXP + e)
                    columns(2 * b, 2 * par + b).then_inc(M["h_ps"], 1)

            def outputs(half, par, last=False):
                m = 2 * half + par
                pe.wait_ge(w_ready, u0 + 4 * NEXP if last else u0 + 4 * m + 6)
                pe.wait_ge(M["hl"], which * (HB * NEXP) + 2 * m + 2)
                for t in range(NT):
                    pe.wait_ge(M["yfree"][t % 4], which * (2 * NEXP) + 2 * m + t // 4)
                    for b in range(HB):
                        got = three_pass(pe, [PS[:, 4 + t % 4, :]], HH[:, par, b, t * P:(t + 1) * P],
                                         HL[:, par, b, t * P:(t + 1) * P], [WH[:, 4 + 2 * par + b, :]],
                                         [WL[:, 4 + 2 * par + b, :]], b == 0, b == HB - 1)
                    if t < NT - 1:
                        got.then_inc(M["y_ps"], 1)
                    else:
                        got.then_inc(M["w2used"][par], 1)

            hidden(0, 0, first=True)
            pe.wait_ge(M["gates"], which + 1)
            for t in range(NT):
                got = pe.transpose(PS[0:NEXP, 4 + t // 4, (t % 4) * P:(t % 4 + 1) * P], gates[:, t, :], ident[:, :])
            got.then_inc(M["gt_ps"], 1)
            pe.wait_ge(M["gt"], which + 1)
            for t in range(NT):
                if t >= 4:
                    pe.wait_ge(M["acc"], which * NT + t - 3)
                pe.matmul(PS[:, 4 + t % 4, :], gatesT[:, t * P:(t + 1) * P], b2[:, which, :],
                          start=True, stop=True).then_inc(M["g_ps"], 1)
            pe.wait_ge(M["acc"], which * NT + NT)
            with pe.Fori(0, NEXP // 2 - 1) as i:
                hidden(i, 1)
                outputs(i, 0)
                hidden(i + 1, 0)
                outputs(i, 1)
            hidden(NEXP // 2 - 1, 1)
            outputs(NEXP // 2 - 1, 0)
            outputs(NEXP // 2 - 1, 1, last=True)

        moe(1, 0, LN["xn"], NT, U_FFN0)

        for b in range(4):
            pe.wait_ge(M["yfree"][b], 2 * NEXP)
        for t in range(NT):
            pe.wait_ge(G["lo"], t + 1)
            pe.wait_ge(G["clo"], t + 1)
            ch = [CGH[:, t % 2, h * HALF:(h + 1) * HALF] for h in range(2)]
            cl = [CGL[:, t % 2, h * HALF:(h + 1) * HALF] for h in range(2)]
            for k in range(KT):
                got = three_pass(pe, two_banks(2 * k), XNH[:, t, k * P:(k + 1) * P], XNL[:, t, k * P:(k + 1) * P],
                                 ch, cl, t == 0, t == NT - 1)
            got.then_inc(G["ps"], 1)
        pe.wait_ge(G["rt_lo"], KT)
        with pe.Fori(0, 2) as g:
            for n in range(4):
                pe.wait_ge(w_ready, U_GNN + 8 * g + n + 1)
                pe.wait_ge(G["relu"][n % 2], 2 * g + n // 2)
                columns(2 * (n % 2), n).then_inc(G["h_ps"], 1)
            pe.wait_ge(w_ready, U_GNN + 8 * g + 8)
            for par in range(2):
                pe.wait_ge(G["ml"][par], 2 * g + 2)
            for t in range(NT):
                pe.wait_ge(G["yfree"][t % 4], 2 * g + t // 4)
                for n in range(4):
                    got = three_pass(pe, [PS[:, 4 + t % 4, :]], MH[:, n, t * P:(t + 1) * P], ML[:, n, t * P:(t + 1) * P],
                                     [WH[:, 4 + n, :]], [WL[:, 4 + n, :]], n == 0, n == 3)
                got.then_inc(G["y_ps"], 1)

        transposes(2, XN, LN["xn"], 3 * NT)
        pe.wait_ge(TR["done"], NT * 3)

        def heads(hp):
            items = 2 * NT * hp
            pe.wait_ge(w_ready, U_ATT + 4 * hp + 1)
            for b in range(2):
                pe.wait_ge(B["yfree"][b], 2 * hp)
            columns(0, 0).then_inc(B["q_ps"], 1)
            pe.wait_ge(w_ready, U_ATT + 4 * hp + 2)
            for b in range(2, 4):
                pe.wait_ge(B["yfree"][b], 2 * hp)
            columns(2, 1).then_inc(B["k_ps"], 1)
            pe.wait_ge(w_ready, U_ATT + 4 * hp + 3)
            pe.wait_ge(B["t_lo"], items)
            for t in range(NT):
                q = slice(t * P, (t + 1) * P)
                for k in range(KT):
                    got = three_pass(pe, [banks(4)[:, q]], XTH[:, k, q], XTL[:, k, q], [wblk(WH, 2, k)], [wblk(WL, 2, k)],
                                     k == 0, k == KT - 1)
            got.then_inc(B["v_ps"], 1)
            pe.wait_ge(B["q_lo"], hp + 1)
            pe.wait_ge(B["k_lo"], hp + 1)

            def scores(m):
                h, t = (m // 2) % 2, 2 * (m // 4) + m % 2
                r = slice(h * DH, (h + 1) * DH)
                if m >= 2:
                    pe.wait_ge(B["exp"], items + m - 1)
                three_pass(pe, two_banks(2 * (m % 2)), AQH[r, t * P:(t + 1) * P], AQL[r, t * P:(t + 1) * P],
                           [AKH[r, i * HALF:(i + 1) * HALF] for i in range(2)],
                           [AKL[r, i * HALF:(i + 1) * HALF] for i in range(2)], True, True).then_inc(B["s_ps"], 1)

            def p_transposes(m):
                pe.wait_ge(B["norm"], items + m + 1)
                if m:
                    pe.wait_ge(B["t_lo"], items + m)
                for k in range(NT):
                    got = pe.transpose(banks(4)[:, k * P:(k + 1) * P], AP_[:, m % 4, k * P:(k + 1) * P], ident[:, :])
                got.then_inc(B["t_ps"], 1)

            def values(g):
                qp, h = g // 2, g % 2
                pe.wait_ge(B["t_lo"], items + 2 * g + 2)
                if qp >= 2 and h == 0:
                    pe.wait_ge(B["cx_lo"], 4 * hp + qp - 1)
                for k in range(NT):
                    got = three_pass(pe, [PS[:, 6 + qp % 2, 0:2 * P]], AVH[:, k, h, :], AVL[:, k, h, :],
                                     [APH[:, g % 2, k, :]], [APL[:, g % 2, k, :]], h == 0 and k == 0, h == 1 and k == NT - 1)
                got.then_inc(B["pv_ps"], 1)

            scores(0)
            scores(1)
            pe.wait_ge(B["v_lo"], 2 * hp + 2)
            for m in range(2 * NT):
                p_transposes(m)
                if m + 2 < 2 * NT:
                    scores(m + 2)
                if m % 2 and m >= 3:
                    values((m - 1) // 2 - 1)
            values(NT - 1)
            pe.wait_ge(w_ready, U_ATT + 4 * hp + 4)
            for t in range(NT):
                pe.wait_ge(B["exp"], items + 2 * NT)
                pe.wait_ge(B["cx_lo"], 4 * hp + t // 2 + 1)
                if t >= 4:
                    pe.wait_ge(B["yfree"][t % 4], 2 * hp + 1)
                q = slice(t * P, (t + 1) * P)
                three_pass(pe, [PS[:, t % 4, :]], CXH[:, q], CXL[:, q], [WH[:, 3, :]], [WL[:, 3, :]],
                           True, True).then_inc(B["y_ps"], 1)

        with pe.Fori(0, KT) as hp:
            heads(hp)

        moe(3, 1, F["n1"], 0, U_MOE1)


_INS = ["x", "src", "dst"] + ["L0_gnn_" + n for n in ("Wq", "bq", "Wk", "bk", "Wv", "bv")] + \
    ["L0_ffn_" + n for n in ("gate_w", "gate_b", "w1", "b1", "w2", "b2")] + \
    ["L1_gnn_" + n for n in ("W1", "b1", "W2", "b2", "eps")] + \
    ["L1_ffn_" + n for n in ("Wq", "bq", "Wk", "bk", "Wv", "bv", "Wo", "bo", "g1", "beta1", "g2", "beta2",
                             "Wg", "bg", "W1", "b1", "W2", "b2")]


def kernel(**inputs):
    import numpy as np
    import concourse.bacc as bacc
    from concourse.bass_utils import run_bass_kernel_spmd
    from contextlib import ExitStack

    nc = bacc.Bacc("TRN2", target_bir_lowering=False, num_devices=1)
    arrays, aps = {}, {}
    for name in _INS:
        array = np.ascontiguousarray(inputs[name])
        arrays["in_" + name] = array
        aps[name] = nc.dram_tensor("in_" + name, array.shape, mybir.dt.from_np(array.dtype), kind="ExternalInput").ap()
    out = nc.dram_tensor("out_0", (1024, 512), F32, kind="ExternalOutput").ap()
    with ExitStack() as ctx:
        build(nc, aps, out, ctx)
    result = run_bass_kernel_spmd(nc, [arrays], core_ids=[0])
    return result.results[0]["out_0"]
```

```python
import concourse.bass as bass
from concourse import mybir

F32 = mybir.dt.float32
F32R = mybir.dt.float32r
F16 = mybir.dt.float16
I32 = mybir.dt.int32
U32 = mybir.dt.uint32
ALU = mybir.AluOpType
ACT = mybir.ActivationFunctionType
X_AXIS = mybir.AxisListType.X
Copy, Identity = ACT.Copy, ACT.Identity

P = 128


def ds(i, n=1):
    return bass.ds(i, n)


def build(nc, a, out, ctx):
    N, D = a["x"].shape
    NE = a["src"].shape[0]
    NT, KT = N // P, D // P
    HALF = N // 2
    EC = NE // P
    NEXP, _, HID = a["L0_ffn_w1"].shape
    HB = HID // P
    GB = a["L1_gnn_W1"].shape[1] // P
    NH, DH = 8, D // 8
    NEG = 1000000.0
    TABLES = 4
    QUADS = EC // 4
    assert EC % 4 == 0 and HB == 2 and GB == 8 and NT == 8 and KT == 4

    place = [((nc.sbuf_base + 31) // 32) * 32]

    def const(name, shape, dt):
        size = 2 if dt == F16 else 4
        for s in shape[1:]:
            size *= s
        t = nc.alloc_sbuf_tensor_at(name, shape, dt, offset=place[0])
        place[0] += (size + 31) // 32 * 32
        return t

    ident = const("ident", [P, P], F32)
    ident16 = const("ident16", [P, P], F16)
    ident1024 = const("ident1024", [P, P], F16)
    earlier = const("earlier", [P, P], F32)
    spare = const("spare", [P, 1], F32)
    index_s = const("index_s", [P, 2, 4], U32)
    count_s = const("count_s", [P, 2, 4], F32)
    stats = const("stats", [P, NT, 6], F32)
    mv = const("mv", [P, NT, 2], F32)
    ve, rstd, inv, sq = (const(n, [P, NT], F32) for n in ("ve", "rstd", "inv", "sq"))
    bq0 = const("bq0", [P, KT], F32)
    bk0 = const("bk0", [P, KT], F32)
    b1_0 = const("b1_0", [P, NEXP * HB], F32)
    gb1 = const("gb1", [P, GB], F32)
    bq1 = const("bq1", [P, KT], F32)
    bq1s = const("bq1s", [P, KT], F32)
    bk1 = const("bk1", [P, KT], F32)
    bv1 = const("bv1", [P, KT], F32)
    b1_1 = const("b1_1", [P, NEXP * HB], F32)
    gw = const("gw", [P, 2, KT, NEXP], F32)
    gwh = const("gwh", [P, 2, KT, NEXP], F32R)
    gwl = const("gwl", [P, 2, KT, NEXP], F32R)
    gbias = const("gbias", [P, 2, NEXP], F32)
    eps1 = const("eps1", [P, 2], F32)
    b2 = const("b2", [NEXP, 2, D], F32)
    row0 = const("row0", [P, D], F32)
    gates = const("gates", [P, NT, NEXP], F32)
    gtmp = const("gtmp", [P, NT, NEXP], F32)
    gsum = const("gsum", [P, NT], F32)
    lower = const("lower", [P, NEXP, NEXP], F32)
    gatesT = const("gatesT", [NEXP, N], F32)
    neg_max = const("neg_max", [P, 4], F32)
    denom = const("denom", [P, 4], F32)
    rden = const("rden", [P, 4], F32)

    RAW = const("RAW", [P, 4, D], F32)
    WH = const("WH", [P, 8, D], F32R)
    wl_offset = place[0]
    WL = const("WL", [P, 8, D], F32R)
    X = const("X", [P, NT, D], F32)

    A0 = place[0]
    K = 1024

    def f(t):
        return t.bitcast(F32)

    def arena(name, shape, dt, kb):
        return nc.alloc_sbuf_tensor_at(name, shape, dt, offset=A0 + int(kb * K))

    XTH = arena("XTH", [P, KT, N], F32R, 0)
    XTL = arena("XTL", [P, KT, N], F32R, 16)
    SR = arena("SR", [P, NT, N], F32, 0)
    QH = arena("QH", [P, KT, N], F32R, 32)
    QL = arena("QL", [P, KT, N], F32R, 48)
    KH = arena("KH", [P, KT, N], F32R, 64)
    KL = arena("KL", [P, KT, N], F32R, 80)
    VH = arena("VH", [P, NT, D], F32R, 96)
    VL = arena("VL", [P, NT, D], F32R, 112)
    XN0 = arena("XN0", [P, NT, D], F32, 96)
    zeros = arena("zeros", [P, 2048], F32, 112)
    CT = arena("CT", [P, 2, TABLES, N], F32, 32)
    PR = arena("PR", [P, 2, N], F32, 64)
    PTH = arena("PTH", [P, 2, N], F32R, 72)
    PTL = arena("PTL", [P, 2, N], F32R, 80)
    src_i = arena("src_i", [P, EC], I32, 120)
    dst_i = arena("dst_i", [P, EC], I32, 121)
    junk = arena("junk", [P, 2, 4, P], F32, 122)
    src16 = arena("src16", [P, EC], F16, 128)
    dst16 = arena("dst16", [P, EC], F16, 128.5)
    key = arena("key", [P, EC], F32, 129)
    key_spare = arena("key_spare", [P, EC], F32, 130)
    multi = arena("multi", [P, EC], F32, 131)
    index = arena("index", [P, EC], U32, 132)
    count = arena("count", [P, EC], F32, 133)
    moved = arena("moved", [P, EC], F32, 134)
    XN = arena("XN", [P, NT, D], F32, 32)
    HF = arena("HF", [P, HB, N], F32, 48)
    HH = arena("HH", [P, 2, HB, N], F32R, 56)
    HL = arena("HL", [P, 2, HB, N], F32R, 72)
    cmp4 = arena("cmp4", [P, 2, NT, NEXP, NEXP], F32, 88)
    XNH = arena("XNH", [P, NT, D], F32R, 48)
    XNL = arena("XNL", [P, NT, D], F32R, 64)
    CG = arena("CG", [P, 2, N], F32, 80)
    CGH = arena("CGH", [P, 2, N], F32R, 88)
    CGL = arena("CGL", [P, 2, N], F32R, 96)
    MF = arena("MF", [P, 2, N], F32, 80)
    MH = arena("MH", [P, 4, N], F32R, 48)
    ML = arena("ML", [P, 4, N], F32R, 64)
    AQH = arena("AQH", [P, 2, N], F32R, 48)
    AQL = arena("AQL", [P, 2, N], F32R, 56)
    AKH = arena("AKH", [P, N], F32R, 64)
    AKL = arena("AKL", [P, N], F32R, 68)
    AVH = arena("AVH", [P, NT, 2, P], F32R, 72)
    AVL = arena("AVL", [P, NT, 2, P], F32R, 80)
    AP_ = arena("AP_", [P, 4, N], F32, 88)
    APH = arena("APH", [P, NT, HALF], F32R, 104)
    APL = arena("APL", [P, NT, HALF], F32R, 120)
    CXH = WH[:, 4:6, :].rearrange("p a b -> p (a b)")
    CXL = WH[:, 6:8, :].rearrange("p a b -> p (a b)")
    VF = nc.alloc_sbuf_tensor_at("VF", [P, N], F32, offset=wl_offset + 4 * D * 4)
    rows1 = arena("rows1", [P, 4, D], F32, 112)
    assert A0 + 136 * K <= nc.sbuf_usable_end, (A0, nc.sbuf_usable_end)

    PS = nc.alloc_psum_tensor("PS", [P, 8, 512], F32)

    def banks(b, n=2):
        return PS[:, b:b + n, :].rearrange("p a b -> p (a b)")

    tables = [nc.dram_tensor(f"edge_table{r}", (N * N + P, 1), F32, kind="Internal").ap() for r in range(TABLES)]
    counts_d = nc.dram_tensor("counts", (N, N), F32, kind="Internal").ap()

    WO_BANKS = (2, 3, 6, 7)

    def sem(name):
        return nc.alloc_semaphore(name)

    x_in, edges_in, cols0_in, cols_in = sem("x_in"), sem("edges_in"), sem("cols0_in"), sem("cols_in")
    row0_in, row0b_in, rows1_in = sem("row0_in"), sem("row0b_in"), sem("rows1_in")
    zeros_set, tables_clear = sem("zeros_set"), [sem(f"table{r}_clear") for r in range(TABLES)]
    setup = sem("setup")
    keys_cast, keys_dve = sem("keys_cast"), sem("keys_dve")
    keyrow_ps, keyrow_used = sem("keyrow_ps"), [sem(f"keyrow_used{i}") for i in range(2)]
    dedup_dve, edges_ready = sem("dedup_dve"), sem("edges_ready")
    staged, scattered = sem("staged"), [sem(f"scattered{r}") for r in range(TABLES)]
    raw_in = [sem(f"raw_in{s}") for s in range(4)]
    w_hi, w_ready = sem("w_hi"), sem("w_ready")
    gw_hi, gw_ready = sem("gw_hi"), sem("gw_ready")

    def stage_semaphores(stage, names, **rings):
        one = {n: sem(f"{stage}_{n}") for n in names.split()}
        more = {n: [sem(f"{stage}_{n}{i}") for i in range(k)] for n, k in rings.items()}
        return {**one, **more}

    LN = stage_semaphores("norm", "dve var root xn")
    TR = stage_semaphores("xt", "ps hi done")
    Q0 = stage_semaphores("qkv0", "ps hi v_ps v_hi v_done s_ps s_done bias", lo=2)
    A = stage_semaphores("att0", "sum1 summed penalty m1 m2 mx exp rden stored", c_in=2, t_ps=2, t_hi=2, t_lo=2, av_ps=2, done=2)
    M = stage_semaphores("moe", "lg_ps gate_dve shifted g_exp gates gt_ps gt g_ps acc h_ps hh hl y_ps", w2used=2, gelu=2, yfree=4)
    G = stage_semaphores("gnn", "hi lo eps diag chi clo ps rt_hi rt_lo h_ps mh y_ps featsum", c_in=2, relu=2, ml=2, yfree=4)
    B = stage_semaphores("att1", "zeroed bq scaled q_ps q_hi q_lo k_ps k_hi k_lo v_ps v_f vt_ps v_hi v_lo s_ps mx exp rden norm "
                         "cx_hi cx_lo y_ps bias", t_ps=2, t_hi=2, t_lo=2, pv_ps=2, yfree=4)
    row0c_in = sem("row0c_in")
    F = stage_semaphores("fin", "g1 n1 g2 n2 done out")

    wq = {0: a["L0_gnn_Wq"], 1: a["L1_ffn_Wq"]}
    wk = {0: a["L0_gnn_Wk"], 1: a["L1_ffn_Wk"]}

    def colblock(w, n):
        return w.rearrange("(k p) n -> p k n", p=P)[:, :, ds(n * P, P)]

    U_FFN0 = 12
    U_GNN = U_FFN0 + 4 * NEXP
    U_ATT = U_GNN + 2 * GB
    U_MOE1 = U_ATT + 16

    def raw3(s):
        return RAW[:, s, :].rearrange("p (k n) -> p k n", k=KT)

    def wblk(t, s, k):
        return t[:, s, k * P:(k + 1) * P]

    def three_pass(pe, outs, lh, ll, rh, rl, first, last):
        for lhs, rhs, j in ((lh, rh, 0), (lh, rl, 1), (ll, rh, 2)):
            for o, r in zip(outs, rhs):
                got = pe.matmul(o, lhs, r, start=first and j == 0, stop=last and j == 2)
        return got

    def halves(t, k):
        return [t[:, k, h * HALF:(h + 1) * HALF] for h in range(2)]

    block = ctx.enter_context(nc.Block())

    @block.sync
    def _(sp):
        def wait(s, value):
            sp.wait_ge(s, value)
            if not isinstance(value, int):
                sp.nop(nofuse=True)

        def load(u, dst_ap, src_ap, s, j):
            if j is None or j >= 4:
                wait(w_ready, u - 3)
            sp.dma_start(dst_ap, src_ap).then_inc(raw_in[s], 16)

        pt = "(p c) -> p c"
        sp.dma_start(src_i[:, :], a["src"].rearrange(pt, p=P)).then_inc(edges_in, 16)
        sp.dma_start(dst_i[:, :], a["dst"].rearrange(pt, p=P)).then_inc(edges_in, 16)
        sp.dma_start(X[:, :, :], a["x"].rearrange("(t p) d -> p t d", p=P)).then_inc(x_in, 16)
        with nc.allow_non_contiguous_dma(reason="biases, one feature per partition"):
            sp.dma_start(bq0[:, :], a["L0_gnn_bq"].rearrange("(k p) -> p k", p=P)).then_inc(cols0_in, 16)
            sp.dma_start(bk0[:, :], a["L0_gnn_bk"].rearrange("(k p) -> p k", p=P)).then_inc(cols0_in, 16)
        for u in range(4):
            load(u, raw3(u), colblock((wq, wk)[u % 2][0], u // 2), u, u)
        wait(zeros_set, 1)
        for r in range(TABLES):
            sp.dma_start(tables[r][0:N * N, :].rearrange("(p c f) o -> p c (f o)", p=P, c=4),
                         zeros[:, :].unsqueeze(1).to_broadcast([P, 4, 2048])).then_inc(tables_clear[r], 16)
            sp.dma_start(tables[r][N * N:N * N + P, :], zeros[:, 0:1]).then_inc(tables_clear[r], 16)
        for u in range(4, 8):
            load(u, raw3(u % 4), colblock((wq, wk)[u % 2][0], u // 2), u % 4, u)
        for k in range(KT):
            load(8 + k, RAW[:, k, :], a["L0_gnn_Wv"][k * P:(k + 1) * P, :], k, 8 + k)
        sp.dma_start(row0[:, :], a["L0_gnn_bv"].partition_broadcast(P)).then_inc(row0_in, 16)
        with nc.allow_non_contiguous_dma(reason="biases, one feature per partition"):
            for t, n in ((gb1, "L1_gnn_b1"), (bq1, "L1_ffn_bq"), (bk1, "L1_ffn_bk"), (bv1, "L1_ffn_bv")):
                sp.dma_start(t[:, :], a[n].rearrange("(k p) -> p k", p=P)).then_inc(cols_in, 16)
            for t, n in ((b1_0, "L0_ffn_b1"), (b1_1, "L1_ffn_b1")):
                sp.dma_start(t[:, :], a[n].rearrange("e (k p) -> p (e k)", p=P)).then_inc(cols_in, 16)
            for m, n in enumerate(("L0_ffn_gate_w", "L1_ffn_Wg")):
                sp.dma_start(gw[:, m, :, :], a[n].rearrange("(k p) e -> p k e", p=P)).then_inc(cols_in, 16)
        for m, n in enumerate(("L0_ffn_gate_b", "L1_ffn_bg")):
            sp.dma_start(gbias[:, m, :], a[n].partition_broadcast(P)).then_inc(cols_in, 16)
        for m, n in enumerate(("L0_ffn_b2", "L1_ffn_b2")):
            sp.dma_start(b2[:, m, :], a[n]).then_inc(cols_in, 16)
        sp.dma_start(eps1[:, 0:1], a["L1_gnn_eps"].partition_broadcast(P)).then_inc(cols_in, 16)

        def moe_load(u0, w1, w2):
            def load_w1(e, u, s):
                for b in range(HB):
                    load(u + b, raw3((s + b) % 4),
                         w1[ds(e)].rearrange("a (k p) h -> p (a k) h", p=P)[:, :, b * P:(b + 1) * P], (s + b) % 4, None)

            def load_w2(e, u, s):
                for b in range(HB):
                    load(u + b, RAW[:, (s + b) % 4, :],
                         w2[ds(e)].rearrange("a (k p) h -> p (a k) h", p=P)[:, b, :], (s + b) % 4, None)

            if u0 != U_FFN0:
                load_w1(0, u0, 0)
            with sp.Fori(0, NEXP - 1) as m:
                load_w1(m + 1, u0 + 2 + 4 * m, 2)
                load_w2(m, u0 + 4 + 4 * m, 0)
            load_w2(NEXP - 1, u0 + 4 * NEXP - 2, 2)

        for b in range(HB):
            load(U_FFN0 + b, raw3(b), a["L0_ffn_w1"][0].rearrange("(k p) h -> p k h", p=P)[:, :, b * P:(b + 1) * P], b, None)

        for r in range(TABLES):
            wait(scattered[r], 16 * QUADS)

        def count_in(t, par):
            for r in range(TABLES):
                sp.dma_start(CT[:, par, r, :],
                             tables[r][ds(t * P * N, P * N), :].rearrange("(p f) o -> p (f o)", p=P)).then_inc(A["c_in"][par], 16)

        def count_out(t, par):
            sp.dma_start(counts_d[ds(t * P, P), :], CT[:, par, 0, :]).then_inc(A["stored"], 16)

        wait(Q0["s_done"], NT)
        count_in(0, 0)
        count_in(1, 1)
        with sp.Fori(0, NT // 2 - 1) as i:
            for par in range(2):
                wait(A["summed"], 2 * i + par + 1)
                count_out(2 * i + par, par)
                wait(A["exp"], 2 * i + par + 1)
                wait(A["stored"], 32 * i + 16 * par + 16)
                count_in(2 * i + par + 2, par)
        for t in (NT - 2, NT - 1):
            wait(A["summed"], t + 1)
            count_out(t, t % 2)
        moe_load(U_FFN0, a["L0_ffn_w1"], a["L0_ffn_w2"])

        wait(Q0["bias"], 1)
        sp.dma_start(row0[:, :], a["L1_gnn_b2"].partition_broadcast(P)).then_inc(row0b_in, 16)
        wait(A["stored"], 16 * NT)
        for par in range(2):
            wait(M["w2used"][par], NEXP // 2)

        def gcount_in(t, par):
            sp.dma_start(CG[:, par, :], counts_d[ds(t * P, P), :]).then_inc(G["c_in"][par], 16)

        gcount_in(0, 0)
        gcount_in(1, 1)
        with sp.Fori(0, NT // 2 - 1) as i:
            for par in range(2):
                wait(G["clo"], 2 * i + par + 1)
                gcount_in(2 * i + par + 2, par)
        with sp.Fori(0, 2) as g:
            for n in range(4):
                load(U_GNN + 8 * g + n, raw3(n), colblock(a["L1_gnn_W1"], 4 * g + n), n, None)
            for n in range(4):
                load(U_GNN + 8 * g + 4 + n, RAW[:, n, :], a["L1_gnn_W2"][ds((4 * g + n) * P, P), :], n, None)

        wait(G["featsum"], 1)
        sp.dma_start(row0[:, :], a["L1_ffn_bo"].partition_broadcast(P)).then_inc(row0c_in, 16)

        def qkv_in(hp, u, s):
            for j, n in enumerate(("L1_ffn_Wq", "L1_ffn_Wk", "L1_ffn_Wv")):
                load(u + j, raw3((s + j) % 4), colblock(a[n], hp), (s + j) % 4, None)

        qkv_in(0, U_ATT, 0)
        with sp.Fori(0, KT - 1) as hp:
            load(U_ATT + 3 + 4 * hp, RAW[:, 3, :], a["L1_ffn_Wo"][ds(hp * P, P), :], 3, None)
            qkv_in(hp + 1, U_ATT + 4 + 4 * hp, 0)
        load(U_ATT + 15, RAW[:, 3, :], a["L1_ffn_Wo"][(KT - 1) * P:KT * P, :], 3, None)
        wait(B["y_ps"], NT * KT)
        for j, n in enumerate(("L1_ffn_g1", "L1_ffn_beta1", "L1_ffn_g2", "L1_ffn_beta2")):
            sp.dma_start(rows1[:, j, :], a[n].partition_broadcast(P)).then_inc(rows1_in, 16)
        moe_load(U_MOE1, a["L1_ffn_W1"], a["L1_ffn_W2"])

        for t in range(NT):
            wait(F["done"], t + 1)
            sp.dma_start(out[t * P:(t + 1) * P, :], X[:, t, :]).then_inc(F["out"], 16)
        wait(F["out"], 16 * NT)

    @block.gpsimd
    def _(gp):
        def wait(s, value):
            gp.wait_ge(s, value)
            if not isinstance(value, int):
                gp.nop(nofuse=True)

        gp.memset(zeros[:, :], 0.0).then_inc(zeros_set, 1)
        gp.memset(ident[:, :], 0.0).then_inc(setup, 1)
        gp.memset(ident16[:, :], 0.0).then_inc(setup, 1)
        gp.memset(ident1024[:, :], 0.0).then_inc(setup, 1)
        gp.memset(earlier[:, :], 257.0).then_inc(setup, 1)
        gp.memset(lower[:, :, :], 1.0).then_inc(setup, 1)
        wait(setup, 5)
        for t, v in ((ident, 1.0), (ident16, 1.0), (ident1024, 1024.0)):
            gp.affine_select(out=t[:, :], in_=t[:, :], compare_op=ALU.not_equal, fill=v,
                             base=0, pattern=[[-1, P]], channel_multiplier=1).then_inc(setup, 1)
        gp.affine_select(out=earlier[:, :], in_=earlier[:, :], compare_op=ALU.is_gt, fill=1.0,
                         base=0, pattern=[[-1, P]], channel_multiplier=1).then_inc(setup, 1)
        gp.affine_select(out=lower[:, :, :], in_=lower[:, :, :], compare_op=ALU.is_gt, fill=0.0,
                         base=0, pattern=[[1, NEXP], [-1, NEXP]], channel_multiplier=0).then_inc(setup, 1)
        gp.iota(spare[:, :], pattern=[[0, 1]], base=N * N, channel_multiplier=1,
                allow_small_or_imprecise_dtypes=True).then_inc(setup, 1)

        for r in range(TABLES):
            wait(tables_clear[r], 32)
        with gp.Fori(0, QUADS // 2) as i:
            for par in range(2):
                q = 2 * i + par
                wait(edges_ready, q + 1)
                gp.tensor_copy(index_s[:, par, :], index[:, ds(4 * q, 4)]).then_inc(staged, 1)
                gp.tensor_copy(count_s[:, par, :], count[:, ds(4 * q, 4)]).then_inc(staged, 1)
                wait(staged, 2 * q + 2)
                for r in range(TABLES):
                    wait(scattered[r], 16 * q)
                    gp.indirect_dma_start(
                        out=tables[r], out_offset=bass.IndirectOffsetOnAxis(ap=index_s[:, par, r:r + 1], axis=0),
                        in_=count_s[:, par, r:r + 1], in_offset=None, compute_op=ALU.add).then_inc(scattered[r], 16)

        def split(u, turn, raw, slot, scaled=None):
            wait(raw_in[raw], 16 * (turn + 1))
            if scaled is not None:
                gp.tensor_scalar(RAW[:, raw, :], RAW[:, raw, :], DH ** -0.5, None, ALU.mult).then_inc(B["scaled"], 1)
                wait(B["scaled"], scaled + 1)
            gp.tensor_copy(WH[:, slot, :], RAW[:, raw, :]).then_inc(w_hi, 1)
            wait(w_hi, u + 1)
            gp.tensor_tensor(WL[:, slot, :], RAW[:, raw, :], f(WH[:, slot, :]), ALU.subtract).then_inc(w_ready, 1)

        wait(w_ready, U_FFN0)
        wait(Q0["ps"], 8)
        for b in range(HB):
            split(U_FFN0 + b, U_FFN0 // 4, b, b)

        with gp.Fori(0, NT // 2) as i:
            for par in range(2):
                t = 2 * i + par
                wait(A["c_in"][par], 64 * i + 64)
                gp.tensor_tensor(CT[:, par, 0, :], CT[:, par, 0, :], CT[:, par, 1, :], ALU.add).then_inc(A["sum1"], 1)
                gp.tensor_tensor(CT[:, par, 2, :], CT[:, par, 2, :], CT[:, par, 3, :], ALU.add).then_inc(A["sum1"], 1)
                wait(A["sum1"], 2 * t + 2)
                gp.tensor_tensor(CT[:, par, 0, :], CT[:, par, 0, :], CT[:, par, 2, :], ALU.add).then_inc(A["summed"], 1)
                wait(A["summed"], t + 1)
                gp.tensor_scalar(CT[:, par, 1, :], CT[:, par, 0, :], 1.0, NEG, ALU.min, ALU.mult).then_inc(A["penalty"], 1)

        def moe_split(which, u0, skip_first):
            if not skip_first:
                for b in range(HB):
                    split(u0 + b, u0 // 4, b, b)

            def pair(half, par, last=False):
                m = 2 * half + par
                if not last:
                    wait(M["h_ps"], which * (HB * NEXP) + 2 * m)
                    for b in range(HB):
                        split(u0 + 2 + 4 * m + b, u0 // 4 + m, 2 + b, 2 * (1 - par) + b)
                wait(M["w2used"][par], which * (NEXP // 2) + half)
                for b in range(HB):
                    if last:
                        split(u0 + 4 * NEXP - 2 + b, u0 // 4 + NEXP - 1, 2 + b, 4 + 2 * par + b)
                    else:
                        split(u0 + 4 + 4 * m + b, u0 // 4 + 1 + m, b, 4 + 2 * par + b)

            with gp.Fori(0, NEXP // 2 - 1) as i:
                pair(i, 0)
                pair(i, 1)
            pair(NEXP // 2 - 1, 0)
            pair(NEXP // 2 - 1, 1, last=True)

        wait(Q0["v_ps"], NT)
        moe_split(0, U_FFN0, True)

        wait(M["h_ps"], 2 * NEXP)
        for par in range(2):
            wait(M["w2used"][par], NEXP // 2)
        with gp.Fori(0, 2) as g:
            wait(G["h_ps"], 4 * g)
            for n in range(4):
                split(U_GNN + 8 * g + n, U_GNN // 4 + 2 * g, n, n)
            wait(G["y_ps"], NT * g)
            for n in range(4):
                split(U_GNN + 8 * g + 4 + n, U_GNN // 4 + 2 * g + 1, n, 4 + n)

        wait(G["y_ps"], 2 * NT)
        for t in (AQH, AQL):
            gp.memset(f(t[:, :, :]), 0.0).then_inc(B["zeroed"], 1)
        for t in (AVH, AVL):
            gp.memset(f(t[:, :, :, :]), 0.0).then_inc(B["zeroed"], 1)
        def qkv_split(hp, j):
            if j == 0:
                wait(B["q_ps"], hp)
            elif j == 1:
                wait(B["k_ps"], hp)
            else:
                wait(B["v_ps"], hp)
            split(U_ATT + 4 * hp + j, U_ATT // 4 + hp, j, j, scaled=hp if j == 0 else None)

        for j in range(3):
            qkv_split(0, j)
        with gp.Fori(0, KT - 1) as hp:
            wait(B["y_ps"], NT * hp)
            split(U_ATT + 4 * hp + 3, U_ATT // 4 + hp, 3, 3)
            for j in range(3):
                qkv_split(hp + 1, j)
        wait(B["y_ps"], NT * (KT - 1))
        split(U_ATT + 4 * KT - 1, U_ATT // 4 + KT - 1, 3, 3)

        wait(B["y_ps"], NT * KT)
        moe_split(1, U_MOE1, False)

    @block.scalar
    def _(act):
        def wait(s, value):
            act.wait_ge(s, value)
            if not isinstance(value, int):
                act.nop(nofuse=True)

        def copy(dst, src, s, **kw):
            act.activation(dst, src, Copy, **kw).then_inc(s, 1)

        def root(turn):
            act.wait_ge(LN["var"], turn + 1)
            act.activation(rstd[:, :], ve[:, :], ACT.Sqrt).then_inc(LN["root"], 1)

        def transposed(turn):
            for t in range(NT):
                act.wait_ge(TR["ps"], NT * turn + t + 1)
                copy(XTH[:, :, t * P:(t + 1) * P], PS[:, t % 2, :].rearrange("p (k n) -> p k n", k=KT), TR["hi"])

        def w_hi_of(u, turn, raw, slot):
            act.wait_ge(raw_in[raw], 16 * (turn + 1))
            copy(WH[:, slot, :], RAW[:, raw, :], w_hi)

        root(0)
        for u in range(4):
            w_hi_of(u, 0, u, u)
        transposed(0)
        act.wait_ge(cols0_in, 32)
        with act.Fori(0, 2) as i:
            for j in range(4):
                n = 2 * i + j // 2
                dst, bias = ((QH, bq0), (KH, bk0))[j % 2]
                wait(Q0["ps"], 4 * i + j + 1)
                act.activation(dst[:, ds(n), :].rearrange("p a n -> p (a n)"), banks(2 * (j % 2)), Identity,
                               bias=bias[:, ds(n)]).then_inc(Q0["hi"], 1)
                act.wait_ge(raw_in[j], 16 * i + 32)
                copy(WH[:, ds(4 * i + j), :].rearrange("p a n -> p (a n)"), RAW[:, j, :], w_hi)
        for t in range(NT):
            act.wait_ge(Q0["v_ps"], t + 1)
            copy(VH[:, t, :], PS[:, t % 4, :], Q0["v_hi"])
        for t in range(NT):
            act.wait_ge(Q0["s_ps"], t + 1)
            copy(SR[:, t, :], banks(4 + 2 * (t % 2)), Q0["s_done"], scale=D ** -0.5)

        def softmax(half, par):
            t = 2 * half + par
            act.wait_ge(A["mx"], t + 1)
            act.wait_ge(A["t_ps"][par], half)
            act.activation(PR[:, par, :], CT[:, par, 3, :], ACT.Exp, bias=neg_max[:, par:par + 1],
                           accum_out=denom[:, par:par + 1]).then_inc(A["exp"], 1)

        def p_hi(half, par):
            act.wait_ge(A["t_ps"][par], half + 1)
            act.wait_ge(A["av_ps"][par], half)
            copy(PTH[:, par, :], banks(4 + 2 * par), A["t_hi"][par])

        softmax(0, 0)
        softmax(0, 1)
        p_hi(0, 0)
        with act.Fori(0, NT // 2 - 1) as i:
            softmax(i + 1, 0)
            p_hi(i, 1)
            softmax(i + 1, 1)
            p_hi(i + 1, 0)
        p_hi(NT // 2 - 1, 1)

        def moe(turn, which):
            transposed(turn)
            if which == 0:
                act.wait_ge(cols_in, 16 * 13)
                copy(gwh[:, :, :, :], gw[:, :, :, :], gw_hi)
                act.wait_ge(M["shifted"], 1)
                act.activation(gtmp[:, :, :], gtmp[:, :, :], ACT.Exp).then_inc(M["g_exp"], 1)
            b1 = (b1_0, b1_1)[which]

            def hidden(half, par):
                e = 2 * half + par
                for b in range(HB):
                    act.wait_ge(M["h_ps"], which * (HB * NEXP) + 2 * e + b + 1)
                    wait(M["hl"], which * (HB * NEXP) + 2 * e)
                    act.activation(HF[:, b, :], banks(2 * b), ACT.Gelu,
                                   bias=b1[:, ds(2 * e + b)]).then_inc(M["gelu"][b], 1)
                    act.wait_ge(M["gelu"][b], which * NEXP + e + 1)
                    act.wait_ge(M["w2used"][par], which * (NEXP // 2) + half)
                    copy(HH[:, par, b, :], HF[:, b, :], M["hh"])

            def transposed_gates():
                act.wait_ge(M["gt_ps"], which + 1)
                copy(gatesT[:, :], PS[0:NEXP, 4:6, :].rearrange("p a b -> p (a b)"), M["gt"])

            hidden(0, 0)
            transposed_gates()
            with act.Fori(0, NEXP // 2 - 1) as i:
                hidden(i, 1)
                hidden(i + 1, 0)
            hidden(NEXP // 2 - 1, 1)

        root(1)
        moe(1, 0)

        root(2)
        for t in range(NT):
            act.wait_ge(LN["xn"], NT * 2 + t + 1)
            copy(XNH[:, t, :], XN[:, t, :], G["hi"])
        for t in range(NT):
            act.wait_ge(G["diag"], t + 1)
            if t >= 2:
                act.wait_ge(G["ps"], t - 1)
            copy(CGH[:, t % 2, :], CG[:, t % 2, :], G["chi"])
        act.wait_ge(G["ps"], NT)
        for k in range(KT):
            copy(XTH[:, k, :], banks(2 * k), G["rt_hi"])
        with act.Fori(0, 2) as g:
            for n in range(4):
                act.wait_ge(G["h_ps"], 4 * g + n + 1)
                wait(G["ml"][n % 2], 2 * g + n // 2)
                act.activation(MF[:, n % 2, :], banks(2 * (n % 2)), ACT.Relu,
                               bias=gb1[:, ds(4 * g + n)]).then_inc(G["relu"][n % 2], 1)
                act.wait_ge(G["relu"][n % 2], 2 * g + n // 2 + 1)
                copy(MH[:, n, :], MF[:, n % 2, :], G["mh"])

        root(3)
        transposed(2)
        act.wait_ge(B["bq"], 1)

        def q_hi(hp):
            wait(B["q_ps"], hp + 1)
            for h in range(2):
                r = slice(h * DH, (h + 1) * DH)
                act.activation(AQH[r, h, :], banks(0)[r, :], Identity, bias=bq1s[r, ds(hp)]).then_inc(B["q_hi"], 1)

        def k_hi(hp):
            wait(B["k_ps"], hp + 1)
            act.activation(AKH[:, :], banks(2), Identity, bias=bk1[:, ds(hp)]).then_inc(B["k_hi"], 1)

        def v_copy(hp):
            act.wait_ge(B["v_ps"], hp + 1)
            copy(VF[:, :], banks(4), B["v_f"])

        def v_hi(hp):
            act.wait_ge(B["vt_ps"], hp + 1)
            for h in range(2):
                c = slice(h * DH, (h + 1) * DH)
                copy(AVH[:, :, h, c], banks(4).rearrange("p (t c) -> p t c", t=NT)[:, :, c], B["v_hi"])

        def heads_softmax(hp, m):
            act.wait_ge(B["mx"], 2 * NT * hp + m + 1)
            if m >= 4:
                act.wait_ge(B["t_ps"][1], 2 * NT * hp + m - 3)
            act.activation(AP_[:, m % 4, :], banks(2 * (m % 2)), ACT.Exp, bias=neg_max[:, m % 4:m % 4 + 1],
                           accum_out=denom[:, m % 4:m % 4 + 1]).then_inc(B["exp"], 1)

        def context_hi(hp, c):
            wait(B["pv_ps"][1], 4 * hp + 2 * c + 2)
            act.activation(CXH[:, c * HALF:(c + 1) * HALF], PS[:, 6 + c, :], Identity,
                           bias=bv1[:, ds(hp)]).then_inc(B["cx_hi"], 1)

        def heads(hp, last=False):
            for m in range(2 * NT):
                for half in range(2):
                    if m >= 4:
                        act.wait_ge(B["pv_ps"][half], 4 * hp + m // 4)
                    act.wait_ge(B["t_ps"][half], 2 * NT * hp + m + 1)
                    copy(APH[:, 4 * half:4 * half + 4, (m % 4) * P:(m % 4 + 1) * P],
                         PS[:, 4 + half, :].rearrange("p (k q) -> p k q", k=4), B["t_hi"][half])
                if m + 1 < 2 * NT:
                    heads_softmax(hp, m + 1)
                if m == 9:
                    context_hi(hp, 0)
            if not last:
                q_hi(hp + 1)
                k_hi(hp + 1)
            context_hi(hp, 1)
            if not last:
                v_copy(hp + 1)
                heads_softmax(hp + 1, 0)
                v_hi(hp + 1)

        act.wait_ge(B["zeroed"], 4)
        q_hi(0)
        k_hi(0)
        v_copy(0)
        v_hi(0)
        heads_softmax(0, 0)
        with act.Fori(0, KT - 1) as hp:
            heads(hp)
        heads(KT - 1, last=True)

        root(4)
        moe(3, 1)
        root(5)

    @block.vector
    def _(v):
        def lo(dst, src, hi, s):
            v.tensor_tensor(dst, src, f(hi), ALU.subtract).then_inc(s, 1)

        def lo_biased(dst, src, bias, hi, s):
            v.scalar_tensor_tensor(out=dst, in0=src, scalar=bias, in1=f(hi), op0=ALU.add, op1=ALU.subtract).then_inc(s, 1)

        def layernorm(turn, src, dst):
            done = [turn * (2 * NT + 5)]

            def step(ins):
                ins.then_inc(LN["dve"], 1)
                done[0] += 1

            for t in range(NT):
                step(v.bn_stats(stats[:, t, :], src[:, t, :]))
            for t in range(NT):
                v.wait_ge(LN["dve"], turn * (2 * NT + 5) + t + 1)
                step(v.bn_aggr(mv[:, t, :], stats[:, t, :]))
            v.wait_ge(LN["dve"], done[0])
            v.tensor_scalar(ve[:, :], mv[:, :, 1], 1e-5, None, ALU.add).then_inc(LN["var"], 1)
            v.wait_ge(LN["root"], turn + 1)
            step(v.reciprocal(inv[:, :], rstd[:, :]))
            v.wait_ge(LN["dve"], done[0])
            step(v.tensor_tensor(sq[:, :], inv[:, :], inv[:, :], ALU.mult))
            v.wait_ge(LN["dve"], done[0])
            step(v.tensor_tensor(ve[:, :], sq[:, :], ve[:, :], ALU.mult))
            v.wait_ge(LN["dve"], done[0])
            step(v.tensor_scalar(ve[:, :], ve[:, :], -0.5, 1.5, ALU.mult, ALU.add))
            v.wait_ge(LN["dve"], done[0])
            step(v.tensor_tensor(rstd[:, :], inv[:, :], ve[:, :], ALU.mult))
            v.wait_ge(LN["dve"], done[0])
            for t in range(NT):
                v.tensor_scalar(dst[:, t, :], src[:, t, :], mv[:, t, 0:1], rstd[:, t:t + 1],
                                ALU.subtract, ALU.mult).then_inc(LN["xn"], 1)

        def transposed(turn):
            for t in range(NT):
                v.wait_ge(TR["hi"], NT * turn + t + 1)
                lo(XTL[:, :, t * P:(t + 1) * P], PS[:, t % 2, :].rearrange("p (k n) -> p k n", k=KT),
                   XTH[:, :, t * P:(t + 1) * P], TR["done"])

        v.wait_ge(edges_in, 32)
        v.tensor_copy(src16[:, :], src_i[:, :]).then_inc(keys_cast, 1)
        v.tensor_copy(dst16[:, :], dst_i[:, :]).then_inc(keys_cast, 1)
        v.wait_ge(keys_cast, 2)
        v.scalar_tensor_tensor(out=key[:, :], in0=src16[:, :], scalar=float(N), in1=dst16[:, :],
                               op0=ALU.mult, op1=ALU.add).then_inc(keys_dve, 1)
        v.wait_ge(keys_dve, 1)
        v.wait_ge(setup, 11)
        v.tensor_scalar(key_spare[:, :], key[:, :], spare[:, 0:1], None, ALU.subtract).then_inc(keys_dve, 1)
        v.wait_ge(keys_dve, 2)

        def quad(q, par, turn):
            v.wait_ge(keyrow_used[par], turn)
            v.wait_ge(keyrow_ps, q + 1)
            for c in range(4):
                got = v.scalar_tensor_tensor(out=junk[:, par, c, :], in0=PS[:, 6 + par, c * P:(c + 1) * P],
                                             scalar=key[:, ds(4 * q + c)], in1=earlier[:, :],
                                             op0=ALU.is_equal, op1=ALU.mult, accum_out=multi[:, ds(4 * q + c)])
            got.then_inc(keyrow_used[par], 1)

        def leaders(q, n, chunk, waits):
            for par, w in waits:
                v.wait_ge(keyrow_used[par], w)
            c = ds(4 * q, 4 * n)
            v.scalar_tensor_tensor(out=count[:, c], in0=multi[:, c], scalar=256.0, in1=multi[:, c],
                                   op0=ALU.is_lt, op1=ALU.mult).then_inc(dedup_dve, 1)
            v.scalar_tensor_tensor(out=moved[:, c], in0=multi[:, c], scalar=256.0, in1=key_spare[:, c],
                                   op0=ALU.is_lt, op1=ALU.mult).then_inc(dedup_dve, 1)
            v.wait_ge(dedup_dve, 2 * chunk + 2)
            v.tensor_scalar(index[:, c], moved[:, c], spare[:, 0:1], None, ALU.add).then_inc(edges_ready, n)

        with v.Fori(0, 5) as i:
            quad(2 * i, 0, i)
            quad(2 * i + 1, 1, i)
            leaders(2 * i, 2, i, ((0, i + 1), (1, i + 1)))

        v.wait_ge(x_in, 16)
        layernorm(0, X, XN0)
        for u in range(4):
            v.wait_ge(w_hi, u + 1)
            lo(WL[:, u, :], RAW[:, u, :], WH[:, u, :], w_ready)
        transposed(0)
        with v.Fori(0, 2) as i:
            for j in range(4):
                n = 2 * i + j // 2
                first = 10 + 12 * i + 3 * j
                for c in range(3):
                    quad(first + c, (3 * j + c) % 2, 5 + 6 * i + (3 * j + c) // 2)
                leaders(first, 3, 5 + 4 * i + j, [(p, 6 * i + 5 + (3 * j + 3 + 1 - p) // 2) for p in range(2)])
                dst, hi_, bias = ((QL, QH, bq0), (KL, KH, bk0))[j % 2]
                v.wait_ge(Q0["hi"], 4 * i + j + 1)
                lo_biased(dst[:, ds(n), :].rearrange("p a n -> p (a n)"), banks(2 * (j % 2)), bias[:, ds(n)],
                          hi_[:, ds(n), :].rearrange("p a n -> p (a n)"), Q0["lo"][j % 2])
                v.wait_ge(w_hi, 4 * i + j + 5)
                lo(WL[:, ds(4 * i + j), :].rearrange("p a n -> p (a n)"), RAW[:, j, :],
                   WH[:, ds(4 * i + j), :].rearrange("p a n -> p (a n)"), w_ready)
        for r in range(TABLES):
            v.wait_ge(tables_clear[r], 32)
        for t in range(NT):
            v.wait_ge(Q0["v_hi"], t + 1)
            lo(VL[:, t, :], PS[:, t % 4, :], VH[:, t, :], Q0["v_done"])
        v.wait_ge(row0_in, 16)
        v.tensor_tensor(X[:, :, :], X[:, :, :], row0[:, :].unsqueeze(1).to_broadcast([P, NT, D]), ALU.add).then_inc(Q0["bias"], 1)
        v.wait_ge(Q0["bias"], 1)

        def mask(half, par):
            t = 2 * half + par
            v.wait_ge(A["summed"], t + 1)
            v.wait_ge(Q0["s_done"], NT)
            v.scalar_tensor_tensor(out=CT[:, par, 2, :], in0=CT[:, par, 0, :], scalar=1.0,
                                   in1=SR[:, ds(t), :].rearrange("p a n -> p (a n)"),
                                   op0=ALU.min, op1=ALU.mult).then_inc(A["m1"], 1)
            v.wait_ge(A["m1"], t + 1)
            v.wait_ge(A["penalty"], t + 1)
            v.scalar_tensor_tensor(out=CT[:, par, 3, :], in0=CT[:, par, 1, :], scalar=NEG, in1=CT[:, par, 2, :],
                                   op0=ALU.subtract, op1=ALU.add).then_inc(A["m2"], 1)
            v.wait_ge(A["m2"], t + 1)
            v.tensor_reduce(out=neg_max[:, par:par + 1], in_=CT[:, par, 3, :], axis=X_AXIS, op=ALU.max,
                            negate=True).then_inc(A["mx"], 1)

        def p_lo(half, par):
            v.wait_ge(A["done"][par], half)
            v.wait_ge(A["exp"], 2 * half + par + 1)
            v.reciprocal(rden[:, par:par + 1], denom[:, par:par + 1]).then_inc(A["rden"], 1)
            v.wait_ge(A["t_hi"][par], half + 1)
            lo(PTL[:, par, :], banks(4 + 2 * par), PTH[:, par, :], A["t_lo"][par])

        def residual(half, par):
            t = 2 * half + par
            v.wait_ge(A["av_ps"][par], half + 1)
            v.wait_ge(A["rden"], t + 1)
            x = X[:, ds(t), :].rearrange("p a n -> p (a n)")
            v.scalar_tensor_tensor(out=x, in0=PS[:, par, :], scalar=rden[:, par:par + 1], in1=x,
                                   op0=ALU.mult, op1=ALU.add).then_inc(A["done"][par], 1)

        mask(0, 0)
        mask(0, 1)
        p_lo(0, 0)
        with v.Fori(0, NT // 2 - 1) as i:
            mask(i + 1, 0)
            p_lo(i, 1)
            residual(i, 0)
            mask(i + 1, 1)
            p_lo(i + 1, 0)
            residual(i, 1)
        p_lo(NT // 2 - 1, 1)
        residual(NT // 2 - 1, 0)
        residual(NT // 2 - 1, 1)
        v.wait_ge(A["done"][0], NT // 2)
        v.wait_ge(A["done"][1], NT // 2)

        def moe(turn, which, acc):
            transposed(turn)
            if which == 0:
                v.wait_ge(gw_hi, 1)
                lo(gwl[:, :, :, :], gw[:, :, :, :], gwh[:, :, :, :], gw_ready)
            v.wait_ge(M["lg_ps"], which * NT + NT)
            steps = [10 * which]

            def own(ins):
                ins.then_inc(M["gate_dve"], 1)
                steps[0] += 1

            own(v.tensor_tensor(gtmp[:, :, :], PS[:, 7, 0:NT * NEXP].rearrange("p (t e) -> p t e", t=NT),
                            gbias[:, which, :].unsqueeze(1).to_broadcast([P, NT, NEXP]), ALU.add))
            v.wait_ge(M["gate_dve"], steps[0])

            def wide(t):
                return t.unsqueeze(2).to_broadcast([P, NT, NEXP])

            if which == 0:
                own(v.tensor_reduce(out=gsum[:, :], in_=gtmp[:, :, :], axis=X_AXIS, op=ALU.max))
                v.wait_ge(M["gate_dve"], steps[0])
                v.tensor_tensor(gtmp[:, :, :], gtmp[:, :, :], wide(gsum[:, :]), ALU.subtract).then_inc(M["shifted"], 1)
                v.wait_ge(M["g_exp"], 1)
                own(v.tensor_reduce(out=gsum[:, :], in_=gtmp[:, :, :], axis=X_AXIS, op=ALU.add))
                v.wait_ge(M["gate_dve"], steps[0])
                own(v.reciprocal(gsum[:, :], gsum[:, :]))
                v.wait_ge(M["gate_dve"], steps[0])
                own(v.tensor_tensor(gtmp[:, :, :], gtmp[:, :, :], wide(gsum[:, :]), ALU.mult))
                v.wait_ge(M["gate_dve"], steps[0])
            shape = [P, NT, NEXP, NEXP]
            mine = gtmp[:, :, :].unsqueeze(3).to_broadcast(shape)
            other = gtmp[:, :, :].unsqueeze(2).to_broadcast(shape)
            own(v.tensor_tensor(cmp4[:, 0], other, mine, ALU.is_gt))
            own(v.tensor_tensor(cmp4[:, 1], other, mine, ALU.is_equal))
            v.wait_ge(M["gate_dve"], steps[0])
            own(v.tensor_tensor(cmp4[:, 1], cmp4[:, 1], lower[:, :, :].unsqueeze(1).to_broadcast(shape), ALU.mult))
            v.wait_ge(M["gate_dve"], steps[0])
            own(v.tensor_tensor(cmp4[:, 0], cmp4[:, 0], cmp4[:, 1], ALU.add))
            v.wait_ge(M["gate_dve"], steps[0])
            own(v.tensor_reduce(out=gates[:, :, :], in_=cmp4[:, 0], axis=X_AXIS, op=ALU.add))
            v.wait_ge(M["gate_dve"], steps[0])
            if which == 0:
                v.scalar_tensor_tensor(out=gates[:, :, :], in0=gates[:, :, :], scalar=2.0, in1=gtmp[:, :, :],
                                       op0=ALU.is_lt, op1=ALU.mult).then_inc(M["gates"], 1)
            else:
                v.tensor_scalar(gates[:, :, :], gates[:, :, :], 1.0, None, ALU.is_lt).then_inc(M["gates"], 1)

            def hidden(half, par):
                e = 2 * half + par
                for b in range(HB):
                    v.wait_ge(M["hh"], which * (HB * NEXP) + 2 * e + b + 1)
                    lo(HL[:, par, b, :], HF[:, b, :], HH[:, par, b, :], M["hl"])

            def outputs(half, par):
                m = 2 * half + par
                for t in range(NT):
                    if t < NT - 1:
                        v.wait_ge(M["y_ps"], which * ((NT - 1) * NEXP) + (NT - 1) * m + t + 1)
                    else:
                        v.wait_ge(M["w2used"][par], which * (NEXP // 2) + half + 1)
                    v.scalar_tensor_tensor(out=acc[:, t, :], in0=PS[:, 4 + t % 4, :], scalar=gates[:, t, ds(m)],
                                           in1=acc[:, t, :], op0=ALU.mult, op1=ALU.add).then_inc(M["yfree"][t % 4], 1)

            v.wait_ge(M["gates"], which + 1)
            hidden(0, 0)
            for t in range(NT):
                v.wait_ge(M["g_ps"], which * NT + t + 1)
                v.tensor_tensor(acc[:, t, :], acc[:, t, :], PS[:, 4 + t % 4, :], ALU.add).then_inc(M["acc"], 1)
            v.wait_ge(M["acc"], which * NT + NT)
            with v.Fori(0, NEXP // 2 - 1) as i:
                hidden(i, 1)
                outputs(i, 0)
                hidden(i + 1, 0)
                outputs(i, 1)
            hidden(NEXP // 2 - 1, 1)
            outputs(NEXP // 2 - 1, 0)
            outputs(NEXP // 2 - 1, 1)
            for b in range(4):
                v.wait_ge(M["yfree"][b], which * (2 * NEXP) + 2 * NEXP)

        v.wait_ge(A["stored"], 16 * NT)
        layernorm(1, X, XN)
        moe(1, 0, X)

        layernorm(2, X, XN)
        v.wait_ge(cols_in, 16 * 13)
        v.tensor_scalar(eps1[:, 1:2], eps1[:, 0:1], 1.0, None, ALU.add).then_inc(G["eps"], 1)
        v.wait_ge(G["eps"], 1)

        def diagonal(t):
            v.wait_ge(G["c_in"][t % 2], 16 * (t // 2) + 16)
            c = CG[:, t % 2, t * P:(t + 1) * P]
            v.scalar_tensor_tensor(out=c, in0=ident[:, :], scalar=eps1[:, 1:2], in1=c,
                                   op0=ALU.mult, op1=ALU.add).then_inc(G["diag"], 1)

        for t in range(NT):
            v.wait_ge(G["hi"], t + 1)
            lo(XNL[:, t, :], XN[:, t, :], XNH[:, t, :], G["lo"])
        diagonal(0)
        for t in range(NT):
            if t + 1 < NT:
                diagonal(t + 1)
            v.wait_ge(G["chi"], t + 1)
            lo(CGL[:, t % 2, :], CG[:, t % 2, :], CGH[:, t % 2, :], G["clo"])
        v.wait_ge(row0b_in, 16)
        v.tensor_tensor(XN[:, :, :], XN[:, :, :], row0[:, :].unsqueeze(1).to_broadcast([P, NT, D]), ALU.add).then_inc(G["featsum"], 1)
        v.wait_ge(G["featsum"], 1)
        v.tensor_tensor(X[:, :, :], X[:, :, :], XN[:, :, :], ALU.add).then_inc(G["featsum"], 1)
        for k in range(KT):
            v.wait_ge(G["rt_hi"], k + 1)
            lo(XTL[:, k, :], banks(2 * k), XTH[:, k, :], G["rt_lo"])
        v.wait_ge(G["featsum"], 2)
        with v.Fori(0, 2) as g:
            for n in range(4):
                v.wait_ge(G["mh"], 4 * g + n + 1)
                lo(ML[:, n, :], MF[:, n % 2, :], MH[:, n, :], G["ml"][n % 2])
            for t in range(NT):
                v.wait_ge(G["y_ps"], NT * g + t + 1)
                v.tensor_tensor(X[:, t, :], X[:, t, :], PS[:, 4 + t % 4, :], ALU.add).then_inc(G["yfree"][t % 4], 1)
        for b in range(4):
            v.wait_ge(G["yfree"][b], 4)

        layernorm(3, X, XN)
        v.tensor_scalar(bq1s[:, :], bq1[:, :], DH ** -0.5, None, ALU.mult).then_inc(B["bq"], 1)
        transposed(2)
        v.wait_ge(row0c_in, 16)
        v.tensor_tensor(XN[:, :, :], XN[:, :, :], row0[:, :].unsqueeze(1).to_broadcast([P, NT, D]), ALU.add).then_inc(B["bias"], 1)
        v.wait_ge(B["bias"], 1)
        v.wait_ge(B["bq"], 1)

        def q_lo(hp):
            for h in range(2):
                r = slice(h * DH, (h + 1) * DH)
                v.wait_ge(B["q_hi"], 2 * hp + 2)
                lo_biased(AQL[r, h, :], banks(0)[r, :], bq1s[r, ds(hp)], AQH[r, h, :], B["q_lo"])

        def k_lo(hp):
            v.wait_ge(B["k_hi"], hp + 1)
            lo_biased(AKL[:, :], banks(2), bk1[:, ds(hp)], AKH[:, :], B["k_lo"])

        def v_lo(hp):
            v.wait_ge(B["v_hi"], 2 * hp + 2)
            for h in range(2):
                c = slice(h * DH, (h + 1) * DH)
                lo(AVL[:, :, h, c], banks(4).rearrange("p (t c) -> p t c", t=NT)[:, :, c], AVH[:, :, h, c], B["v_lo"])

        def maximum(hp, m):
            v.wait_ge(B["s_ps"], 2 * NT * hp + m + 1)
            v.tensor_reduce(out=neg_max[:, m % 4:m % 4 + 1], in_=banks(2 * (m % 2)), axis=X_AXIS, op=ALU.max,
                            negate=True).then_inc(B["mx"], 1)

        def normalise(hp, m):
            v.wait_ge(B["exp"], 2 * NT * hp + m + 1)
            if m == 0 or m >= 4:
                v.wait_ge(B["norm"], 2 * NT * hp + max(m - 3, 0))
            v.reciprocal(rden[:, m % 4:m % 4 + 1], denom[:, m % 4:m % 4 + 1]).then_inc(B["rden"], 1)
            v.wait_ge(B["rden"], 2 * NT * hp + m + 1)
            v.tensor_scalar(AP_[:, m % 4, :], AP_[:, m % 4, :], rden[:, m % 4:m % 4 + 1], None,
                            ALU.mult).then_inc(B["norm"], 1)

        def context_lo(hp, c):
            v.wait_ge(B["cx_hi"], 2 * hp + c + 1)
            q = slice(c * HALF, (c + 1) * HALF)
            lo_biased(CXL[:, q], PS[:, 6 + c, :], bv1[:, ds(hp)], CXH[:, q], B["cx_lo"])

        def heads(hp, last=False):
            for m in range(2 * NT):
                for half in range(2):
                    v.wait_ge(B["t_hi"][half], 2 * NT * hp + m + 1)
                    block_ = (slice(None), slice(4 * half, 4 * half + 4), slice((m % 4) * P, (m % 4 + 1) * P))
                    lo(APL[block_], PS[:, 4 + half, :].rearrange("p (k q) -> p k q", k=4), APH[block_], B["t_lo"][half])
                if m + 1 < 2 * NT:
                    normalise(hp, m + 1)
                if m + 2 < 2 * NT:
                    maximum(hp, m + 2)
                if m == 10:
                    context_lo(hp, 0)
            if not last:
                q_lo(hp + 1)
                k_lo(hp + 1)
            context_lo(hp, 1)
            if not last:
                maximum(hp + 1, 0)
                v_lo(hp + 1)
                normalise(hp + 1, 0)
            for t in range(NT):
                v.wait_ge(B["y_ps"], NT * hp + t + 1)
                v.tensor_tensor(XN[:, t, :], XN[:, t, :], PS[:, WO_BANKS[t % 4], :], ALU.add).then_inc(B["yfree"][t % 4], 1)
            if not last:
                maximum(hp + 1, 1)

        q_lo(0)
        k_lo(0)
        v_lo(0)
        maximum(0, 0)
        normalise(0, 0)
        maximum(0, 1)
        with v.Fori(0, KT - 1) as hp:
            heads(hp)
        heads(KT - 1, last=True)
        for b in range(4):
            v.wait_ge(B["yfree"][b], 2 * KT)

        def gain(g, b, g_done, b_done):
            for t in range(NT):
                v.tensor_tensor(XN[:, t, :], XN[:, t, :], rows1[:, g, :], ALU.mult).then_inc(g_done, 1)
            for t in range(NT):
                v.wait_ge(g_done, t + 1)
                v.tensor_tensor(XN[:, t, :], XN[:, t, :], rows1[:, b, :], ALU.add).then_inc(b_done, 1)

        layernorm(4, XN, XN)
        v.wait_ge(rows1_in, 64)
        v.wait_ge(LN["xn"], NT * 5)
        gain(0, 1, F["g1"], F["n1"])
        moe(3, 1, XN)
        layernorm(5, XN, XN)
        v.wait_ge(LN["xn"], NT * 6)
        gain(2, 3, F["g2"], F["n2"])
        for t in range(NT):
            v.wait_ge(F["n2"], t + 1)
            v.tensor_tensor(X[:, t, :], X[:, t, :], XN[:, t, :], ALU.add).then_inc(F["done"], 1)

    @block.tensor
    def _(pe):
        def transposes(turn, src, ready, before):
            for t in range(NT):
                pe.wait_ge(ready, before + t + 1)
                if t >= 2:
                    pe.wait_ge(TR["done"], NT * turn + t - 1)
                for k in range(KT):
                    got = pe.transpose(PS[:, t % 2, k * P:(k + 1) * P], src[:, t, k * P:(k + 1) * P], ident[:, :])
                got.then_inc(TR["ps"], 1)

        def two_banks(b):
            return [PS[:, b, :], PS[:, b + 1, :]]

        def columns(b, slot, th=XTH, tl=XTL):
            for k in range(KT):
                got = three_pass(pe, two_banks(b), wblk(WH, slot, k), wblk(WL, slot, k), halves(th, k), halves(tl, k),
                                 k == 0, k == KT - 1)
            return got

        pe.wait_ge(setup, 11)
        pe.wait_ge(keys_cast, 2)

        def quad(q, par, turn):
            pe.wait_ge(keyrow_used[par], turn)
            for c in range(4):
                o = PS[:, 6 + par, c * P:(c + 1) * P]
                pe.matmul(o, src16[:, ds(4 * q + c)].to_broadcast([P, P]), ident1024[:, :], start=True, stop=False)
                got = pe.matmul(o, dst16[:, ds(4 * q + c)].to_broadcast([P, P]), ident16[:, :], start=False, stop=True)
            got.then_inc(keyrow_ps, 1)

        with pe.Fori(0, 5) as i:
            quad(2 * i, 0, i)
            quad(2 * i + 1, 1, i)

        transposes(0, XN0, LN["xn"], 0)
        pe.wait_ge(TR["done"], NT * 1)
        with pe.Fori(0, 2) as i:
            for j in range(4):
                for c in range(3):
                    quad(10 + 12 * i + 3 * j + c, (3 * j + c) % 2, 5 + 6 * i + (3 * j + c) // 2)
                pe.wait_ge(w_ready, 4 * i + j + 1)
                pe.wait_ge(Q0["lo"][j % 2], 2 * i + j // 2)
                columns(2 * (j % 2), j).then_inc(Q0["ps"], 1)
        pe.wait_ge(w_ready, 12)
        for par in range(2):
            pe.wait_ge(Q0["lo"][par], 4)
        for t in range(NT):
            if t >= 4:
                pe.wait_ge(Q0["v_done"], t - 3)
            q = slice(t * P, (t + 1) * P)
            for k in range(KT):
                got = three_pass(pe, [PS[:, t % 4, :]], XTH[:, k, q], XTL[:, k, q], [WH[:, 4 + k, :]], [WL[:, 4 + k, :]],
                                 k == 0, k == KT - 1)
            got.then_inc(Q0["v_ps"], 1)
        for par in range(2):
            pe.wait_ge(keyrow_used[par], QUADS // 2)
        for t in range(NT):
            if t >= 2:
                pe.wait_ge(Q0["s_done"], t - 1)
            q = slice(t * P, (t + 1) * P)
            for k in range(KT):
                got = three_pass(pe, two_banks(4 + 2 * (t % 2)), QH[:, k, q], QL[:, k, q], halves(KH, k), halves(KL, k),
                                 k == 0, k == KT - 1)
            got.then_inc(Q0["s_ps"], 1)

        def p_transposes(half, par):
            pe.wait_ge(A["exp"], 2 * half + par + 1)
            pe.wait_ge(A["t_lo"][par], half)
            for k in range(NT):
                got = pe.transpose(banks(4 + 2 * par)[:, k * P:(k + 1) * P], PR[:, par, k * P:(k + 1) * P], ident[:, :])
            got.then_inc(A["t_ps"][par], 1)

        def values(half, par):
            pe.wait_ge(A["t_lo"][par], half + 1)
            pe.wait_ge(A["done"][par], half)
            for k in range(NT):
                got = three_pass(pe, [PS[:, par, :]], PTH[:, par, k * P:(k + 1) * P], PTL[:, par, k * P:(k + 1) * P],
                                 [VH[:, k, :]], [VL[:, k, :]], k == 0, k == NT - 1)
            got.then_inc(A["av_ps"][par], 1)

        pe.wait_ge(Q0["s_done"], NT)
        pe.wait_ge(Q0["v_done"], NT)
        p_transposes(0, 0)
        with pe.Fori(0, NT // 2 - 1) as i:
            p_transposes(i, 1)
            values(i, 0)
            p_transposes(i + 1, 0)
            values(i, 1)
        p_transposes(NT // 2 - 1, 1)
        values(NT // 2 - 1, 0)
        values(NT // 2 - 1, 1)

        def moe(turn, which, ready, before, u0):
            transposes(turn, XN, ready, before)
            pe.wait_ge(TR["done"], NT * (turn + 1))
            if which == 0:
                pe.wait_ge(gw_ready, 1)
            for t in range(NT):
                q = slice(t * P, (t + 1) * P)
                for k in range(KT):
                    got = three_pass(pe, [PS[:, 7, t * NEXP:(t + 1) * NEXP]], XTH[:, k, q], XTL[:, k, q],
                                     [gwh[:, which, k, :]], [gwl[:, which, k, :]], k == 0, k == KT - 1)
                got.then_inc(M["lg_ps"], 1)

            def hidden(half, par, first=False):
                e = 2 * half + par
                for b in range(HB):
                    pe.wait_ge(w_ready, u0 + 1 + b if first else u0 + 4 * e - 1 + b)
                    pe.wait_ge(M["gelu"][b], which * NEXP + e)
                    columns(2 * b, 2 * par + b).then_inc(M["h_ps"], 1)

            def outputs(half, par, last=False):
                m = 2 * half + par
                pe.wait_ge(w_ready, u0 + 4 * NEXP if last else u0 + 4 * m + 6)
                pe.wait_ge(M["hl"], which * (HB * NEXP) + 2 * m + 2)
                for t in range(NT):
                    pe.wait_ge(M["yfree"][t % 4], which * (2 * NEXP) + 2 * m + t // 4)
                    for b in range(HB):
                        got = three_pass(pe, [PS[:, 4 + t % 4, :]], HH[:, par, b, t * P:(t + 1) * P],
                                         HL[:, par, b, t * P:(t + 1) * P], [WH[:, 4 + 2 * par + b, :]],
                                         [WL[:, 4 + 2 * par + b, :]], b == 0, b == HB - 1)
                    if t < NT - 1:
                        got.then_inc(M["y_ps"], 1)
                    else:
                        got.then_inc(M["w2used"][par], 1)

            hidden(0, 0, first=True)
            pe.wait_ge(M["gates"], which + 1)
            for t in range(NT):
                got = pe.transpose(PS[0:NEXP, 4 + t // 4, (t % 4) * P:(t % 4 + 1) * P], gates[:, t, :], ident[:, :])
            got.then_inc(M["gt_ps"], 1)
            pe.wait_ge(M["gt"], which + 1)
            for t in range(NT):
                if t >= 4:
                    pe.wait_ge(M["acc"], which * NT + t - 3)
                pe.matmul(PS[:, 4 + t % 4, :], gatesT[:, t * P:(t + 1) * P], b2[:, which, :],
                          start=True, stop=True).then_inc(M["g_ps"], 1)
            pe.wait_ge(M["acc"], which * NT + NT)
            with pe.Fori(0, NEXP // 2 - 1) as i:
                hidden(i, 1)
                outputs(i, 0)
                hidden(i + 1, 0)
                outputs(i, 1)
            hidden(NEXP // 2 - 1, 1)
            outputs(NEXP // 2 - 1, 0)
            outputs(NEXP // 2 - 1, 1, last=True)

        moe(1, 0, LN["xn"], NT, U_FFN0)

        for b in range(4):
            pe.wait_ge(M["yfree"][b], 2 * NEXP)
        for t in range(NT):
            pe.wait_ge(G["lo"], t + 1)
            pe.wait_ge(G["clo"], t + 1)
            ch = [CGH[:, t % 2, h * HALF:(h + 1) * HALF] for h in range(2)]
            cl = [CGL[:, t % 2, h * HALF:(h + 1) * HALF] for h in range(2)]
            for k in range(KT):
                got = three_pass(pe, two_banks(2 * k), XNH[:, t, k * P:(k + 1) * P], XNL[:, t, k * P:(k + 1) * P],
                                 ch, cl, t == 0, t == NT - 1)
            got.then_inc(G["ps"], 1)
        pe.wait_ge(G["rt_lo"], KT)
        with pe.Fori(0, 2) as g:
            for n in range(4):
                pe.wait_ge(w_ready, U_GNN + 8 * g + n + 1)
                pe.wait_ge(G["relu"][n % 2], 2 * g + n // 2)
                columns(2 * (n % 2), n).then_inc(G["h_ps"], 1)
            pe.wait_ge(w_ready, U_GNN + 8 * g + 8)
            for par in range(2):
                pe.wait_ge(G["ml"][par], 2 * g + 2)
            for t in range(NT):
                pe.wait_ge(G["yfree"][t % 4], 2 * g + t // 4)
                for n in range(4):
                    got = three_pass(pe, [PS[:, 4 + t % 4, :]], MH[:, n, t * P:(t + 1) * P], ML[:, n, t * P:(t + 1) * P],
                                     [WH[:, 4 + n, :]], [WL[:, 4 + n, :]], n == 0, n == 3)
                got.then_inc(G["y_ps"], 1)

        transposes(2, XN, LN["xn"], 3 * NT)
        pe.wait_ge(TR["done"], NT * 3)

        def project_q(hp):
            pe.wait_ge(w_ready, U_ATT + 4 * hp + 1)
            columns(0, 0).then_inc(B["q_ps"], 1)

        def project_k(hp):
            pe.wait_ge(w_ready, U_ATT + 4 * hp + 2)
            columns(2, 1).then_inc(B["k_ps"], 1)

        def project_v(hp):
            pe.wait_ge(w_ready, U_ATT + 4 * hp + 3)
            columns(4, 2).then_inc(B["v_ps"], 1)

        def transpose_v(hp):
            pe.wait_ge(B["v_f"], hp + 1)
            for t in range(NT):
                got = pe.transpose(banks(4)[:, t * P:(t + 1) * P], VF[:, t * P:(t + 1) * P], ident[:, :])
            got.then_inc(B["vt_ps"], 1)

        def head_scores(m):
            h, t = (m // 4) % 2, 4 * (m // 8) + m % 4
            q = slice(t * P, (t + 1) * P)
            three_pass(pe, two_banks(2 * (m % 2)), AQH[:, h, q], AQL[:, h, q],
                       [AKH[:, i * HALF:(i + 1) * HALF] for i in range(2)],
                       [AKL[:, i * HALF:(i + 1) * HALF] for i in range(2)], True, True).then_inc(B["s_ps"], 1)

        def heads(hp, last=False):
            items = 2 * NT * hp

            def head_transposes(m):
                pe.wait_ge(B["norm"], items + m + 1)
                for half in range(2):
                    if m:
                        pe.wait_ge(B["t_lo"][half], items + m)
                    for k in range(4):
                        c = 4 * half + k
                        got = pe.transpose(PS[:, 4 + half, k * P:(k + 1) * P], AP_[:, m % 4, c * P:(c + 1) * P], ident[:, :])
                    got.then_inc(B["t_ps"][half], 1)

            def head_values(g, half):
                c, h = g // 2, g % 2
                if h == 0 and half == 0:
                    pe.wait_ge(B["yfree"][2 + c], 2 * hp)
                pe.wait_ge(B["t_lo"][half], items + 4 * g + 4)
                for k in range(4 * half, 4 * half + 4):
                    got = three_pass(pe, [PS[:, 6 + c, :]], AVH[:, k, h, :], AVL[:, k, h, :],
                                     [APH[:, k, :]], [APL[:, k, :]], h == 0 and k == 0, h == 1 and k == NT - 1)
                got.then_inc(B["pv_ps"][half], 1)

            pe.wait_ge(B["v_lo"], 2 * hp + 2)
            for m in range(2 * NT):
                head_transposes(m)
                if m % 4 == 0 and m:
                    head_values(m // 4 - 1, 1)
                if m + 2 < 2 * NT:
                    pe.wait_ge(B["exp"], items + m + 1)
                    head_scores(m + 2)
                if m % 4 == 3 and m < 2 * NT - 1:
                    head_values(m // 4, 0)
                if not last and m == 2 * NT - 2:
                    pe.wait_ge(B["exp"], items + 2 * NT - 1)
                    project_q(hp + 1)
                if not last and m == 2 * NT - 1:
                    pe.wait_ge(B["exp"], items + 2 * NT)
                    project_k(hp + 1)
            head_values(3, 0)
            head_values(3, 1)
            if not last:
                project_v(hp + 1)
                pe.wait_ge(B["q_lo"], 2 * hp + 4)
                pe.wait_ge(B["k_lo"], hp + 2)
                head_scores(0)
                transpose_v(hp + 1)
            pe.wait_ge(w_ready, U_ATT + 4 * hp + 4)
            pe.wait_ge(B["exp"], items + 2 * NT)
            pe.wait_ge(B["cx_lo"], 2 * hp + 2)
            for t in range(NT):
                if t >= 4:
                    pe.wait_ge(B["yfree"][t % 4], 2 * hp + 1)
                q = slice(t * P, (t + 1) * P)
                three_pass(pe, [PS[:, WO_BANKS[t % 4], :]], CXH[:, q], CXL[:, q], [WH[:, 3, :]], [WL[:, 3, :]],
                           True, True).then_inc(B["y_ps"], 1)
            if not last:
                for b in range(2):
                    pe.wait_ge(B["yfree"][b], 2 * hp + 2)
                head_scores(1)

        project_q(0)
        project_k(0)
        project_v(0)
        transpose_v(0)
        pe.wait_ge(B["q_lo"], 2)
        pe.wait_ge(B["k_lo"], 1)
        head_scores(0)
        head_scores(1)
        with pe.Fori(0, KT - 1) as hp:
            heads(hp)
        heads(KT - 1, last=True)

        moe(3, 1, F["n1"], 0, U_MOE1)


_INS = ["x", "src", "dst"] + ["L0_gnn_" + n for n in ("Wq", "bq", "Wk", "bk", "Wv", "bv")] + \
    ["L0_ffn_" + n for n in ("gate_w", "gate_b", "w1", "b1", "w2", "b2")] + \
    ["L1_gnn_" + n for n in ("W1", "b1", "W2", "b2", "eps")] + \
    ["L1_ffn_" + n for n in ("Wq", "bq", "Wk", "bk", "Wv", "bv", "Wo", "bo", "g1", "beta1", "g2", "beta2",
                             "Wg", "bg", "W1", "b1", "W2", "b2")]


def kernel(**inputs):
    import numpy as np
    import concourse.bacc as bacc
    from concourse.bass_utils import run_bass_kernel_spmd
    from contextlib import ExitStack

    nc = bacc.Bacc("TRN2", target_bir_lowering=False, num_devices=1)
    arrays, aps = {}, {}
    for name in _INS:
        array = np.ascontiguousarray(inputs[name])
        arrays["in_" + name] = array
        aps[name] = nc.dram_tensor("in_" + name, array.shape, mybir.dt.from_np(array.dtype), kind="ExternalInput").ap()
    out = nc.dram_tensor("out_0", (1024, 512), F32, kind="ExternalOutput").ap()
    with ExitStack() as ctx:
        build(nc, aps, out, ctx)
    result = run_bass_kernel_spmd(nc, [arrays], core_ids=[0])
    return result.results[0]["out_0"]
```
